# Optimizing a Trainium2 kernel written in Bass

```python
import numpy as np
import jax
import jax.numpy as jnp

def _softmax(x, axis=-1):
    return jax.nn.softmax(x, axis=axis)

def _gelu(x):
    return jax.nn.gelu(x, approximate=True)

def _silu(x):
    return jax.nn.silu(x)

def _sigmoid(x):
    return jax.nn.sigmoid(x)

def _layernorm(x, axis=-1, eps=1e-05):
    m = jnp.mean(x, axis=axis, keepdims=True)
    v = jnp.var(x, axis=axis, keepdims=True)
    return (x - m) / jnp.sqrt(v + eps)

def _scatter_add(tgt, idx, src, axis=0):
    return tgt.at[idx].add(src)

def _segment_sum(src, seg, n):
    return jax.ops.segment_sum(src, seg, n)
kernel_name = 'mk_gnn_resnorm_d4_gnn_r32_1e757e'

def setup_inputs(seed: int=0):
    np.random.seed(seed)
    _w = jnp.asarray

    def _rec_inputs():
        import jax
        import jax.numpy as jnp
        _gk = jax.random.key(seed)
        x = -0.0003713 + 1 * jax.random.normal(jax.random.fold_in(_gk, 1), (50000, 256), jnp.float32)
        src = jax.random.randint(jax.random.fold_in(_gk, 2), (25000,), 0, 50000, jnp.int32)
        dst = jax.random.randint(jax.random.fold_in(_gk, 3), (25000,), 0, 50000, jnp.int32)
        _o = jnp.argsort(dst, stable=True)
        src = src[_o]
        dst = dst[_o]
        edge_attr_256 = 9.41057e-06 + 1 * jax.random.normal(jax.random.fold_in(_gk, 12), (25000, 256), jnp.float32)
        return (x, src, dst, edge_attr_256)
    x, src, dst, edge_attr_256 = _rec_inputs()

    def _L0_gnn_setup():
        import jax, jax.numpy as jnp
        import numpy as np
        N_NODES = 50000
        N_EDGES = 25000
        D_MODEL = 256
        H = 8
        D_K = 32
        key = jax.random.key(seed)
        kx, kq, kk, kv, ks, kd = jax.random.split(key, 6)
        scale = 1.0 / np.sqrt(D_MODEL)
        x = jax.random.normal(kx, (N_NODES, D_MODEL), dtype=jnp.float32)
        Wq = jax.random.normal(kq, (D_MODEL, H * D_K), dtype=jnp.float32) * scale
        Wk = jax.random.normal(kk, (D_MODEL, H * D_K), dtype=jnp.float32) * scale
        Wv = jax.random.normal(kv, (D_MODEL, H * D_K), dtype=jnp.float32) * scale
        src = jax.random.randint(ks, (N_EDGES,), 0, N_NODES, dtype=jnp.int32)
        dst = jax.random.randint(kd, (N_EDGES,), 0, N_NODES, dtype=jnp.int32)
        return {'x': x, 'Wq': Wq, 'Wk': Wk, 'Wv': Wv, 'src': src, 'dst': dst}
    _L0_gnn_all = _L0_gnn_setup()
    _L0_gnn_in = {k: v for k, v in _L0_gnn_all.items() if k in ('Wq', 'Wk', 'Wv')}
    del _L0_gnn_all

    def _L1_gnn_setup():
        import jax, jax.numpy as jnp
        import numpy as np
        N_NODES = 3125
        N_EDGES = 9375
        DIM = 256
        LN_EPS = 1e-05
        key = jax.random.key(seed)
        ks = jax.random.split(key, 4)
        scale = 1.0 / np.sqrt(DIM)
        h = jax.random.normal(ks[0], (N_NODES, DIM), dtype=jnp.float32)
        edge_index = jax.random.randint(ks[1], (2, N_EDGES), 0, N_NODES, dtype=jnp.int64)
        W1 = jax.random.normal(ks[2], (DIM, DIM), dtype=jnp.float32) * scale
        b1 = jnp.zeros((DIM,), dtype=jnp.float32)
        W2 = jax.random.normal(ks[3], (DIM, DIM), dtype=jnp.float32) * scale
        b2 = jnp.zeros((DIM,), dtype=jnp.float32)
        eps = jnp.zeros((), dtype=jnp.float32)
        gamma = jnp.ones((DIM,), dtype=jnp.float32)
        beta = jnp.zeros((DIM,), dtype=jnp.float32)
        return {'h': h, 'edge_index': edge_index, 'W1': W1, 'b1': b1, 'W2': W2, 'b2': b2, 'eps': eps, 'gamma': gamma, 'beta': beta}
    _L1_gnn_all = _L1_gnn_setup()
    _L1_gnn_in = {k: v for k, v in _L1_gnn_all.items() if k in ('W1', 'b1', 'W2', 'b2', 'eps', 'gamma', 'beta')}
    del _L1_gnn_all

    def _L2_gnn_setup():
        import jax, jax.numpy as jnp
        import numpy as np
        N, D, H = (50000, 256, 8)
        C = D // H
        E = 50000
        NEG_SLOPE = 0.2
        EPS = 1e-05

        def _gat_block(x, src, dst, W, att_src, att_dst, bias, ln_w, ln_b):
            n = x.shape[0]
            h = (x @ W).reshape(n, H, C)
            a_src = jnp.einsum('nhc,hc->nh', h, att_src)
            a_dst = jnp.einsum('nhc,hc->nh', h, att_dst)
            e = a_src[src] + a_dst[dst]
            e = jnp.where(e > 0, e, NEG_SLOPE * e)
            m = jax.ops.segment_max(e, dst, num_segments=n)
            m = jnp.where(jnp.isfinite(m), m, 0.0)
            ex = jnp.exp(e - m[dst])
            denom = jax.ops.segment_sum(ex, dst, num_segments=n)
            alpha = ex / denom[dst]
            msg = h[src] * alpha[..., None]
            out = jax.ops.segment_sum(msg, dst, num_segments=n).reshape(n, H * C) + bias
            y = out + x
            mu = y.mean(axis=-1, keepdims=True)
            var = y.var(axis=-1, keepdims=True)
            return (y - mu) / jnp.sqrt(var + EPS) * ln_w + ln_b
        key = jax.random.key(seed)
        ks = jax.random.split(key, 8)
        x = jax.random.normal(ks[0], (N, D), dtype=jnp.float32)
        edge_index = jax.random.randint(ks[1], (2, E), 0, N, dtype=jnp.int32)
        scale = 1.0 / np.sqrt(D)
        W = jax.random.normal(ks[2], (D, H * C), dtype=jnp.float32) * scale
        att_src = jax.random.normal(ks[3], (H, C), dtype=jnp.float32) * scale
        att_dst = jax.random.normal(ks[4], (H, C), dtype=jnp.float32) * scale
        bias = jnp.zeros((H * C,), dtype=jnp.float32)
        ln_w = jnp.ones((D,), dtype=jnp.float32)
        ln_b = jnp.zeros((D,), dtype=jnp.float32)
        return {'x': x, 'edge_index': edge_index, 'W': W, 'att_src': att_src, 'att_dst': att_dst, 'bias': bias, 'ln_w': ln_w, 'ln_b': ln_b}
    _L2_gnn_all = _L2_gnn_setup()
    _L2_gnn_in = {k: v for k, v in _L2_gnn_all.items() if k in ('W', 'att_src', 'att_dst', 'bias', 'ln_w', 'ln_b')}
    del _L2_gnn_all

    def _L3_gnn_setup():
        import jax, jax.numpy as jnp
        import numpy as np
        N, E, NIN, H, C = (50000, 25000, 256, 8, 32)
        HC = H * C
        key = jax.random.key(seed)
        ks = jax.random.split(key, 12)
        s = 0.05
        x = jax.random.normal(ks[0], (N, NIN), dtype=jnp.float32)
        edge_index = jax.random.randint(ks[1], (2, E), 0, N, dtype=jnp.int64)
        edge_attr = jax.random.normal(ks[2], (E, NIN), dtype=jnp.float32)
        Wq = jax.random.normal(ks[3], (NIN, HC), dtype=jnp.float32) * s
        bq = jax.random.normal(ks[4], (HC,), dtype=jnp.float32) * s
        Wk = jax.random.normal(ks[5], (NIN, HC), dtype=jnp.float32) * s
        bk = jax.random.normal(ks[6], (HC,), dtype=jnp.float32) * s
        Wv = jax.random.normal(ks[7], (NIN, HC), dtype=jnp.float32) * s
        bv = jax.random.normal(ks[8], (HC,), dtype=jnp.float32) * s
        We = jax.random.normal(ks[9], (NIN, HC), dtype=jnp.float32) * s
        Ws = jax.random.normal(ks[10], (NIN, HC), dtype=jnp.float32) * s
        bs = jax.random.normal(ks[11], (HC,), dtype=jnp.float32) * s
        return {'x': x, 'edge_index': edge_index, 'edge_attr': edge_attr, 'Wq': Wq, 'bq': bq, 'Wk': Wk, 'bk': bk, 'Wv': Wv, 'bv': bv, 'We': We, 'Ws': Ws, 'bs': bs}
    _L3_gnn_all = _L3_gnn_setup()
    _L3_gnn_in = {k: v for k, v in _L3_gnn_all.items() if k in ('Wq', 'bq', 'Wk', 'bk', 'Wv', 'bv', 'We', 'Ws', 'bs')}
    del _L3_gnn_all
    return {'x': x, 'src': src, 'dst': dst, 'edge_attr_256': edge_attr_256, 'L0_gnn_Wq': _L0_gnn_in['Wq'], 'L0_gnn_Wk': _L0_gnn_in['Wk'], 'L0_gnn_Wv': _L0_gnn_in['Wv'], 'L1_gnn_W1': _L1_gnn_in['W1'], 'L1_gnn_b1': _L1_gnn_in['b1'], 'L1_gnn_W2': _L1_gnn_in['W2'], 'L1_gnn_b2': _L1_gnn_in['b2'], 'L1_gnn_eps': _L1_gnn_in['eps'], 'L1_gnn_gamma': _L1_gnn_in['gamma'], 'L1_gnn_beta': _L1_gnn_in['beta'], 'L2_gnn_W': _L2_gnn_in['W'], 'L2_gnn_att_src': _L2_gnn_in['att_src'], 'L2_gnn_att_dst': _L2_gnn_in['att_dst'], 'L2_gnn_bias': _L2_gnn_in['bias'], 'L2_gnn_ln_w': _L2_gnn_in['ln_w'], 'L2_gnn_ln_b': _L2_gnn_in['ln_b'], 'L3_gnn_Wq': _L3_gnn_in['Wq'], 'L3_gnn_bq': _L3_gnn_in['bq'], 'L3_gnn_Wk': _L3_gnn_in['Wk'], 'L3_gnn_bk': _L3_gnn_in['bk'], 'L3_gnn_Wv': _L3_gnn_in['Wv'], 'L3_gnn_bv': _L3_gnn_in['bv'], 'L3_gnn_We': _L3_gnn_in['We'], 'L3_gnn_Ws': _L3_gnn_in['Ws'], 'L3_gnn_bs': _L3_gnn_in['bs']}

def reference(x, src, dst, edge_attr_256, L0_gnn_Wq, L0_gnn_Wk, L0_gnn_Wv, L1_gnn_W1, L1_gnn_b1, L1_gnn_W2, L1_gnn_b2, L1_gnn_eps, L1_gnn_gamma, L1_gnn_beta, L2_gnn_W, L2_gnn_att_src, L2_gnn_att_dst, L2_gnn_bias, L2_gnn_ln_w, L2_gnn_ln_b, L3_gnn_Wq, L3_gnn_bq, L3_gnn_Wk, L3_gnn_bk, L3_gnn_Wv, L3_gnn_bv, L3_gnn_We, L3_gnn_Ws, L3_gnn_bs):
    import jax
    import jax.numpy as jnp

    def _L0_gnn_ref(x, Wq, Wk, Wv, src, dst):
        import jax, jax.numpy as jnp
        import numpy as np
        N_NODES = 50000
        N_EDGES = 25000
        D_MODEL = 256
        H = 8
        D_K = 32
        q = (x @ Wq).reshape(N_NODES, H, D_K)
        k = (x @ Wk).reshape(N_NODES, H, D_K)
        v = (x @ Wv).reshape(N_NODES, H, D_K)
        score = jnp.sum(k[src] * q[dst], axis=-1, keepdims=True)
        score = jnp.exp(jnp.clip(score / np.sqrt(D_K), -5.0, 5.0))
        wv = jax.ops.segment_sum(v[src] * score, dst, num_segments=N_NODES)
        z = jax.ops.segment_sum(score, dst, num_segments=N_NODES)
        out = wv / (z + 1e-09)
        return out.reshape(N_NODES, H * D_K)

    def _L1_gnn_ref(h, edge_index, W1, b1, W2, b2, eps, gamma, beta):
        import jax, jax.numpy as jnp
        import numpy as np
        N_NODES = 3125
        N_EDGES = 9375
        DIM = 256
        LN_EPS = 1e-05
        src, dst = (edge_index[0], edge_index[1])
        agg = jax.ops.segment_sum(h[src], dst, num_segments=h.shape[0])
        z = (1.0 + eps) * h + agg
        z = jax.nn.relu(z @ W1 + b1) @ W2 + b2
        r = z + h
        mu = jnp.mean(r, axis=-1, keepdims=True)
        var = jnp.mean(jnp.square(r - mu), axis=-1, keepdims=True)
        ln = (r - mu) * jax.lax.rsqrt(var + LN_EPS) * gamma + beta
        return jax.nn.relu(ln)

    def _L2_gnn_ref(x, edge_index, W, att_src, att_dst, bias, ln_w, ln_b):
        import jax, jax.numpy as jnp
        import numpy as np
        N, D, H = (50000, 256, 8)
        C = D // H
        E = 50000
        NEG_SLOPE = 0.2
        EPS = 1e-05

        def _gat_block(x, src, dst, W, att_src, att_dst, bias, ln_w, ln_b):
            n = x.shape[0]
            h = (x @ W).reshape(n, H, C)
            a_src = jnp.einsum('nhc,hc->nh', h, att_src)
            a_dst = jnp.einsum('nhc,hc->nh', h, att_dst)
            e = a_src[src] + a_dst[dst]
            e = jnp.where(e > 0, e, NEG_SLOPE * e)
            m = jax.ops.segment_max(e, dst, num_segments=n)
            m = jnp.where(jnp.isfinite(m), m, 0.0)
            ex = jnp.exp(e - m[dst])
            denom = jax.ops.segment_sum(ex, dst, num_segments=n)
            alpha = ex / denom[dst]
            msg = h[src] * alpha[..., None]
            out = jax.ops.segment_sum(msg, dst, num_segments=n).reshape(n, H * C) + bias
            y = out + x
            mu = y.mean(axis=-1, keepdims=True)
            var = y.var(axis=-1, keepdims=True)
            return (y - mu) / jnp.sqrt(var + EPS) * ln_w + ln_b
        n = x.shape[0]
        loop = jnp.arange(n, dtype=edge_index.dtype)
        src = jnp.concatenate([edge_index[0], loop])
        dst = jnp.concatenate([edge_index[1], loop])
        return _gat_block(x, src, dst, W, att_src, att_dst, bias, ln_w, ln_b)

    def _L3_gnn_ref(x, edge_index, edge_attr, Wq, bq, Wk, bk, Wv, bv, We, Ws, bs):
        import jax, jax.numpy as jnp
        import numpy as np
        N, E, NIN, H, C = (50000, 25000, 256, 8, 32)
        HC = H * C
        src, dst = (edge_index[0], edge_index[1])
        n = x.shape[0]
        q = (x @ Wq + bq).reshape(n, H, C)
        k = (x @ Wk + bk).reshape(n, H, C)
        v = (x @ Wv + bv).reshape(n, H, C)
        e = (edge_attr @ We).reshape(-1, H, C)
        k_j = k[src] + e
        v_j = v[src] + e
        q_i = q[dst]
        alpha = jnp.sum(q_i * k_j, axis=-1) / jnp.sqrt(jnp.float32(C))
        amax = jax.ops.segment_max(alpha, dst, num_segments=n)
        ex = jnp.exp(alpha - amax[dst])
        denom = jax.ops.segment_sum(ex, dst, num_segments=n)
        alpha = ex / denom[dst]
        out = jax.ops.segment_sum(v_j * alpha[:, :, None], dst, num_segments=n)
        out = out.reshape(n, HC)
        out = out + x @ Ws + bs
        return out
    edge_index = jnp.stack([src, dst])
    x = _layernorm(x + _L0_gnn_ref(x, L0_gnn_Wq, L0_gnn_Wk, L0_gnn_Wv, src, dst), axis=-1)
    x = _layernorm(x + _L1_gnn_ref(x, edge_index, L1_gnn_W1, L1_gnn_b1, L1_gnn_W2, L1_gnn_b2, L1_gnn_eps, L1_gnn_gamma, L1_gnn_beta), axis=-1)
    x = _layernorm(x + _L2_gnn_ref(x, edge_index, L2_gnn_W, L2_gnn_att_src, L2_gnn_att_dst, L2_gnn_bias, L2_gnn_ln_w, L2_gnn_ln_b), axis=-1)
    x = _layernorm(x + _L3_gnn_ref(x, edge_index, edge_attr_256, L3_gnn_Wq, L3_gnn_bq, L3_gnn_Wk, L3_gnn_bk, L3_gnn_Wv, L3_gnn_bv, L3_gnn_We, L3_gnn_Ws, L3_gnn_bs), axis=-1)
    return x

_drawn_inputs = setup_inputs


def setup_inputs(seed=0):
    import zlib

    import numpy as np

    out = dict(_drawn_inputs(seed))
    spreads = {'L1_gnn_b1': (0.0, 0.316),
     'L1_gnn_b2': (0.0, 0.1),
     'L1_gnn_gamma': (1.0, 0.2),
     'L1_gnn_beta': (0.0, 0.1),
     'L2_gnn_bias': (0.0, 0.1),
     'L2_gnn_ln_w': (1.0, 0.2),
     'L2_gnn_ln_b': (0.0, 0.1)}
    factors = {'L2_gnn_att_dst': 6.395, 'L3_gnn_bq': 8.0, 'L3_gnn_bk': 8.0, 'L3_gnn_bv': 3.121}
    for name, (base, spread) in spreads.items():
        noise = np.random.default_rng([zlib.crc32(name.encode()), seed]).standard_normal(out[name].shape)
        drawn = base * np.exp(spread * noise) if base else spread * noise
        out[name] = jnp.asarray(drawn.astype(out[name].dtype))
    for name, factor in factors.items():
        out[name] = (out[name] * factor).astype(out[name].dtype)
    return out
```

```python
from contextlib import ExitStack

import concourse.bass as bass
from concourse import mybir

F32 = mybir.dt.float32
BF16 = mybir.dt.bfloat16
I32 = mybir.dt.int32
ALU = mybir.AluOpType
ACT = mybir.ActivationFunctionType
AX = mybir.AxisListType

P = 128
D = 256
H = 8
C = D // H
KC = D // P
N = 50000
E = 25000
EC = -(-E // P)
EPAD = EC * P
ESPILL = EPAD + P
UNITS = -(-N // (2 * P))
TILES = 2 * UNITS
NPAD = TILES * P
LAST_ROWS = N - (TILES - 2) * P
assert 0 < LAST_ROWS < P
NO_NODE = 65535
SKIP = 1 << 20
BIG = 1.0e30
LN_EPS = 1e-5
HI, LO = 13, 32
assert HI * LO > TILES
WB = TILES // 4



def num(piece):
    times, unroll, first = piece
    return first if times is None else times * unroll + first


def ring(piece, size):
    return piece[2] % size


def turn(piece, size):
    times, unroll, first = piece
    return first // size if times is None else times * (unroll // size) + first // size


def had(piece, k):
    return piece[0] is not None or piece[2] >= k


def is_last(piece, total):
    return piece[0] is None and piece[2] == total - 1


def run_steps(eng, total, depth, body, unroll=8):
    head = -(-(depth + 8) // unroll) * unroll
    loops = (total - head) // unroll - 1

    def fixed(s):
        def at(lag):
            return (None, unroll, s - lag) if 0 <= s - lag < total else None
        return at

    for s in range(head):
        body(fixed(s))
    with eng.Fori(0, loops) as times:
        for j in range(unroll):
            body(lambda lag: (times, unroll, head + j - lag))
    for s in range(head + loops * unroll, total + depth):
        body(fixed(s))


def run_range(eng, low, high, body, unroll=4):
    head = -(-(low + 4) // unroll) * unroll
    loops = (high - head) // unroll
    for s in range(low, head):
        body((None, unroll, s))
    with eng.Fori(0, loops) as times:
        for j in range(unroll):
            body((times, unroll, head + j))
    for s in range(head + loops * unroll, high):
        body((None, unroll, s))


def build(nc, a, out):
    top = ExitStack()
    with top:
        _build(nc, a, out, top)


def _build(nc, a, out, top):
    def dram(name, shape, dt=F32):
        return nc.dram_tensor(name, shape, dt).ap()

    def keep(name, shape, dt=F32):
        return top.enter_context(nc.sbuf_tensor(name, shape, dt))

    edge_pairs = dram("edge_pairs", [ESPILL, 2], I32)
    targets = dram("targets", [ESPILL + 2, 1], I32)
    first_edges = dram("first_edges", [HI * LO], I32)
    windows = dram("windows", [TILES, 2 * P], I32)
    x1_d = dram("x1_d", [NPAD, D])
    x2_d = dram("x2_d", [NPAD, D])
    x3_d = dram("x3_d", [NPAD, D])
    h_d = dram("h_d", [NPAD, D])
    att_d = dram("att_d", [NPAD, 2 * H])
    msg0_d = dram("msg0_d", [ESPILL, D + H])
    msg3_d = dram("msg3_d", [ESPILL, D])
    share2_d = dram("share2_d", [ESPILL, 2 * H])
    share3_d = dram("share3_d", [ESPILL, H])

    def by_column(table):
        return table[0:EPAD, :].rearrange("(p c) w -> p c w", c=EC)

    def by_unit(table):
        return table.rearrange("(u h p) w -> p u h w", h=2, p=P)

    ident = keep("ident", [P, P])
    ones = keep("ones", [P, P])
    iota = keep("iota", [P, P])
    eps_ln = keep("eps_ln", [P, 1])
    edge_rows = keep("edge_rows", [P, EC, 2], I32)
    first_row = keep("first_row", [1, HI * LO], I32)
    tile_base = keep("tile_base", [P, TILES])
    target_rel = keep("target_rel", [P, TILES])
    source_row = keep("source_row", [P, TILES], I32)
    join_prev = keep("join_prev", [P, EC])
    join_next = keep("join_next", [P, EC])
    keep_prev = keep("keep_prev", [P, EC])
    first_mark = keep("first_mark", [P, EC])
    chain_max = keep("chain_max", [H, P])
    chain_sum = keep("chain_sum", [H, P])
    chain_next = keep("chain_next", [H, P])
    scores = keep("scores", [P, EC, H])
    w0_kv = keep("w0_kv", [P, KC, 2 * D])
    w0_q = keep("w0_q", [P, KC, D])
    w1_a = keep("w1_a", [P, KC, D])
    w1_b = keep("w1_b", [P, KC, D])
    w2_h = keep("w2_h", [P, KC, D + 2 * H])
    w3_kv = keep("w3_kv", [P, KC, 2 * D])
    w3_q = keep("w3_q", [P, KC, D])
    w3_e = keep("w3_e", [P, KC, D])
    w3_s = keep("w3_s", [P, KC, D])
    att = keep("att", [P, 2, D])
    rows = {n: keep("row_" + n, [P, D]) for n in
            ("L1_gnn_b2", "L1_gnn_gamma", "L1_gnn_beta", "L2_gnn_bias", "L2_gnn_ln_w", "L2_gnn_ln_b", "L3_gnn_bs")}
    b1 = keep("b1", [P, KC])
    gin = keep("gin", [P, 1])
    bias3 = keep("bias3", [3, 3 * D], BF16)
    ones3 = keep("ones3", [3, P], BF16)

    def stage(body, tag):
        used = []
        with ExitStack() as ctx:
            def sb(name, shape, dt=F32):
                return ctx.enter_context(nc.sbuf_tensor(f"{tag}_{name}", shape, dt))

            def ps(name, banks=1):
                shape = [P, 512] if banks == 1 else [P, banks, 512]
                return ctx.enter_context(nc.psum_tensor(f"{tag}_{name}", shape, F32))

            def sem(name):
                used.append(nc.alloc_semaphore(f"{tag}_{name}"))
                return used[-1]

            def sems(name, n):
                return [sem(f"{name}{k}") for k in range(n)]
            body(sb, ps, sem, sems, nc.Block)
            nc.clear_and_free_semaphores(used)
            nc.all_engine_barrier()

    def gate(eng, spare, sem, value):
        eng.wait_ge(sem, value)
        eng.sem_inc(spare, 1)

    def chained(eng, sem):
        count = [0]

        def link(ins):
            count[0] += 1
            ins.then_inc(sem, 1)
            eng.wait_ge(sem, count[0])
        return link

    def prepare(sb, ps, sem, sems, block):
        dst_i = sb("dst_i", [P, EC], I32)
        tile_i = sb("tile_i", [P, EC], I32)
        part_i = sb("part_i", [P, EC], I32)
        hi_f = sb("hi_f", [P, EC])
        lo_f = sb("lo_f", [P, EC])
        below_hi = sb("below_hi", [P, EC * HI + P], BF16)
        at_hi = sb("at_hi", [P, EC * HI + P], BF16)
        below_lo = sb("below_lo", [P, EC, LO], BF16)
        ones_lo = sb("ones_lo", [P, LO], BF16)
        first_f = sb("first_f", [HI, LO], I32)
        pad_pairs = sb("pad_pairs", [P, 2], I32)
        zeros = sb("zeros", [P, D + H])
        near = sb("near", [P, EC + 2], I32)
        near_f = sb("near_f", [P, EC + 2])
        ends = sb("ends", [P, 3])
        ends8 = sb("ends8", [P, 3, H])
        wprod = sb("wprod", [P, D])
        watt = sb("watt", [P, KC, 2 * H])
        b3 = sb("b3", [3, 3 * D])
        b3_part = sb("b3_part", [3, 3 * D], BF16)
        b3_sum = sb("b3_sum", [3, 3 * D])
        cnt_ps, tr2_ps = ps("cnt"), ps("tr2")
        padded, edges_in, weights_in, zeroed = sem("padded"), sems("edges_in", 4), sem("weights_in"), sem("zeroed")
        iotas, paired, pairs_out, masks, counted = sem("iotas"), sem("paired"), sem("pairs_out"), sem("masks"), sem("counted")
        first_cast, first_out, first_in = sem("first_cast"), sem("first_out"), sem("first_in")
        near_in, d, pl = sem("near_in"), sem("d"), sem("pl")
        ends_ready, ends_turned = sem("ends_ready"), sem("ends_turned")

        def row(ap, n, parts=P):
            return bass.AP(ap.tensor, ap.offset, [[0, parts], [1, n]])

        with block() as blk:
            n_loads = [0]

            @blk.sync
            def _(sp):
                def load(dst, src):
                    sp.dma_start(dst, src).then_inc(weights_in, 16)
                    n_loads[0] += 1
                sp.wait_ge(padded, 1)
                whole = (P - 1) * EC
                src, dst = a["src"], a["dst"]
                sp.dma_start(part_i[0:P - 1, :], src[0:whole].rearrange("(p c) -> p c", c=EC)).then_inc(edges_in[0], 16)
                sp.dma_start(part_i[P - 1:P, 0:E - whole], src[whole:E].rearrange("(p c) -> p c", p=1)).then_inc(edges_in[1], 16)
                sp.dma_start(dst_i[0:P - 1, :], dst[0:whole].rearrange("(p c) -> p c", c=EC)).then_inc(edges_in[2], 16)
                sp.dma_start(dst_i[P - 1:P, 0:E - whole], dst[whole:E].rearrange("(p c) -> p c", p=1)).then_inc(edges_in[3], 16)
                for dst_t, name, at in ((w0_kv, "L0_gnn_Wk", 0), (w0_kv, "L0_gnn_Wv", D), (w0_q, "L0_gnn_Wq", 0),
                                        (w1_a, "L1_gnn_W1", 0), (w1_b, "L1_gnn_W2", 0), (w2_h, "L2_gnn_W", 0),
                                        (w3_kv, "L3_gnn_Wk", 0), (w3_kv, "L3_gnn_Wv", D), (w3_q, "L3_gnn_Wq", 0),
                                        (w3_e, "L3_gnn_We", 0), (w3_s, "L3_gnn_Ws", 0)):
                    load(dst_t[:, :, at:at + D], a[name].rearrange("(k p) n -> p k n", p=P))
                for name, t in rows.items():
                    load(t[:, :], row(a[name], D))
                for k, name in enumerate(("L2_gnn_att_src", "L2_gnn_att_dst")):
                    load(att[:, k, :], row(a[name], D))
                for k, name in enumerate(("L3_gnn_bk", "L3_gnn_bv", "L3_gnn_bq")):
                    load(b3[:, k * D:(k + 1) * D], row(a[name], D, 3))
                load(gin[:, :], row(a["L1_gnn_eps"], 1))
                with nc.allow_non_contiguous_dma(reason="256 biases, one to a partition"):
                    load(b1[:, :], a["L1_gnn_b1"].rearrange("(k p) -> p k", p=P))
                sp.wait_ge(paired, 1)
                sp.dma_start(edge_pairs[0:EPAD, :].rearrange("(p c) w -> p (c w)", c=EC), near_pairs[:, :, :]
                             .rearrange("p c w -> p (c w)")).then_inc(pairs_out, 16)
                sp.dma_start(edge_pairs[EPAD:ESPILL, :], pad_pairs[:, :]).then_inc(pairs_out, 16)
                sp.dma_start(targets[1:EPAD + 1, :].rearrange("(p c) w -> p (c w)", c=EC), dst_i[:, :]).then_inc(pairs_out, 16)
                sp.dma_start(targets[0:1, :], pad_pairs[0:1, 0:1]).then_inc(pairs_out, 16)
                sp.dma_start(targets[EPAD + 1:EPAD + 2, :], pad_pairs[0:1, 0:1]).then_inc(pairs_out, 16)
                sp.wait_ge(zeroed, 1)
                for table, width in ((msg0_d, D + H), (msg3_d, D), (share2_d, 2 * H), (share3_d, H)):
                    sp.dma_start(table[EPAD:ESPILL, :], zeros[:, 0:width]).then_inc(pairs_out, 16)
                sp.wait_ge(pairs_out, 9 * 16)
                sp.dma_start(near[:, :], bass.AP(targets.tensor, 0, [[EC, P], [1, EC + 2]])).then_inc(near_in, 16)
                sp.wait_ge(first_cast, 1)
                sp.dma_start(first_edges.rearrange("(a b) -> a b", a=HI), first_f[:, :]).then_inc(first_out, 16)
                sp.wait_ge(first_out, 16)
                sp.dma_start(first_row[:, :], first_edges.rearrange("(a b) -> a b", a=1)).then_inc(first_in, 16)
                sp.wait_ge(first_in, 16)

            @blk.gpsimd
            def _(gp):
                link = chained(gp, pl)
                gp.memset(ident[:, :], 0.0).then_inc(pl, 1)
                gp.memset(ones[:, :], 1.0)
                gp.wait_ge(pl, 1)
                gp.affine_select(out=ident[:, :], in_=ident[:, :], compare_op=ALU.not_equal, fill=1.0, base=0,
                                 pattern=[[-1, P]], channel_multiplier=1)
                gp.iota(iota[:, :], pattern=[[1, P]], base=0, channel_multiplier=0, allow_small_or_imprecise_dtypes=True)
                gp.iota(tile_base[:, :], pattern=[[P, TILES]], base=0, channel_multiplier=0,
                        allow_small_or_imprecise_dtypes=True).then_inc(iotas, 1)

            @blk.vector
            def _(ve):
                link = chained(ve, d)
                nc.vector.memset(part_i[:, :], 0)
                nc.vector.memset(dst_i[:, :], NO_NODE).then_inc(padded, 1)
                link(nc.vector.memset(pad_pairs[:, :], NO_NODE))
                nc.vector.memset(zeros[:, :], 0.0).then_inc(zeroed, 1)
                nc.vector.memset(eps_ln[:, :], LN_EPS)
                nc.vector.memset(ones3[:, :], 1.0)
                nc.vector.memset(ones_lo[:, :], 1.0)
                nc.vector.memset(below_hi[:, :], 0.0)
                link(nc.vector.memset(at_hi[:, :], 0.0))
                for k in range(4):
                    ve.wait_ge(edges_in[k], 16)
                nc.vector.tensor_copy(near_pairs[:, :, 0], part_i[:, :])
                link(nc.vector.tensor_copy(near_pairs[:, :, 1], dst_i[:, :]))
                ve.sem_inc(paired, 1)
                nc.vector.tensor_copy(edge_rows[:, :, 0], part_i[:, :])
                nc.vector.tensor_scalar(edge_rows[:, :, 1], dst_i[:, :], float(N - 1), None, ALU.min)
                link(nc.vector.tensor_scalar(tile_i[:, :], dst_i[:, :], 7, None, ALU.arith_shift_right))
                link(nc.vector.tensor_scalar(part_i[:, :], tile_i[:, :], 5, None, ALU.arith_shift_right))
                link(nc.vector.tensor_copy(hi_f[:, :], part_i[:, :]))
                link(nc.vector.tensor_scalar(part_i[:, :], tile_i[:, :], LO - 1, None, ALU.bitwise_and))
                link(nc.vector.tensor_copy(lo_f[:, :], part_i[:, :]))
                ve.wait_ge(iotas, 1)
                for mask, width, f, op in ((below_hi, HI, hi_f, ALU.is_lt), (at_hi, HI, hi_f, ALU.is_equal)):
                    link(nc.vector.tensor_tensor(
                        mask[:, 0:EC * HI].rearrange("p (c w) -> p c w", w=HI),
                        f[:, :].unsqueeze(2).to_broadcast([P, EC, HI]),
                        iota[:, 0:HI].unsqueeze(1).to_broadcast([P, EC, HI]), op))
                nc.vector.tensor_tensor(below_lo[:, :, :], lo_f[:, :].unsqueeze(2).to_broadcast([P, EC, LO]),
                                        iota[:, 0:LO].unsqueeze(1).to_broadcast([P, EC, LO]), ALU.is_lt).then_inc(masks, 1)
                ve.wait_ge(counted, 1)
                nc.vector.tensor_copy(first_f[:, :], cnt_ps[0:HI, 0:LO]).then_inc(first_cast, 1)
                ve.wait_ge(near_in, 16)
                link(nc.vector.tensor_copy(near_f[:, :], near[:, :]))
                mid = near_f[:, 1:EC + 1]
                nc.vector.tensor_tensor(keep_prev[:, :], mid, near_f[:, 0:EC], ALU.is_equal)
                link(nc.vector.tensor_tensor(join_next[:, :], mid, near_f[:, 2:EC + 2], ALU.is_equal))
                nc.vector.tensor_scalar(first_mark[:, :], keep_prev[:, :], -1.0, 1.0, ALU.mult, ALU.add)
                nc.vector.tensor_scalar(join_prev[:, :], keep_prev[:, :], BIG, -BIG, ALU.mult, ALU.add)
                link(nc.vector.tensor_scalar(join_next[:, :], join_next[:, :], BIG, -BIG, ALU.mult, ALU.add))
                for k, t in enumerate((join_prev, keep_prev, join_next)):
                    link(nc.vector.tensor_reduce(ends[:, k:k + 1], t[:, :], axis=AX.X, op=ALU.min))
                nc.vector.tensor_copy(ends8[:, :, :], ends[:, :].unsqueeze(2).to_broadcast([P, 3, H])).then_inc(ends_ready, 1)
                for k, t in enumerate((chain_max, chain_sum, chain_next)):
                    ve.wait_ge(ends_turned, 1)
                    link(nc.vector.tensor_copy(t[:, :], tr2_ps[0:H, k * P:(k + 1) * P]))
                ve.wait_ge(weights_in, 16 * 25)
                for k in range(KC):
                    for j in range(2):
                        link(nc.vector.tensor_tensor(wprod[:, :], w2_h[:, k, 0:D], att[:, j, :], ALU.mult))
                        link(nc.vector.tensor_reduce(watt[:, k, j * H:(j + 1) * H],
                                                     wprod[:, :].rearrange("p (h c) -> p h c", h=H), axis=AX.X, op=ALU.add))
                link(nc.vector.tensor_copy(w2_h[:, :, D:D + 2 * H], watt[:, :, :]))
                link(nc.vector.tensor_scalar(gin[:, :], gin[:, :], 1.0, None, ALU.add))
                for k in range(3):
                    link(nc.vector.tensor_copy(b3_part[:, :], b3[:, :]))
                    link(nc.vector.tensor_tensor(b3[:, :], b3[:, :], b3_part[:, :], ALU.subtract))
                    if k == 0:
                        link(nc.vector.tensor_scalar(b3_sum[:, :], b3_part[:, :], ident[0:3, 0:1], None, ALU.mult))
                    else:
                        link(nc.vector.scalar_tensor_tensor(b3_sum[:, :], b3_part[:, :], ident[0:3, k:k + 1], b3_sum[:, :],
                                                            ALU.mult, ALU.add))
                link(nc.vector.tensor_copy(bias3[:, :], b3_sum[:, :]))

            @blk.tensor
            def _(pe):
                pe.wait_ge(masks, 1)

                def count(at_c, lo_c, start, stop):
                    nc.tensor.matmul(cnt_ps[:, 0:LO], below_hi[:, at_c], ones_lo[:, :], start=start, stop=False)
                    return nc.tensor.matmul(cnt_ps[:, 0:LO], at_hi[:, at_c], lo_c, start=False, stop=stop)

                count(slice(0, P), below_lo[:, 0, :], True, False)
                with pe.Fori(1, EC - 1) as c:
                    count(bass.ds(c * HI, P), below_lo[:, :, :].rearrange("p c w -> p (c w)")[:, bass.ds(c * LO, LO)], False, False)
                count(slice((EC - 1) * HI, (EC - 1) * HI + P), below_lo[:, EC - 1, :], False, True).then_inc(counted, 1)
                pe.wait_ge(ends_ready, 1)
                for k in range(3):
                    last = nc.tensor.transpose(tr2_ps[0:H, k * P:(k + 1) * P], ends8[:, k, :], ident[:, :])
                last.then_inc(ends_turned, 1)

            assert n_loads[0] == 25, n_loads

    near_pairs = keep("edge_pairs_sb", [P, EC, 2], I32)

    def edges0(sb, ps, sem, sems, block):
        cur = sb("cur", [P, 4, 2], I32)
        xg = sb("xg", [P, 4, 2, D])
        xT = sb("xT", [P, 2, 2, KC, P])
        qs = sb("qs", [P, 2, D])
        prod = sb("prod", [P, 2, D])
        dots = sb("dots", [P, 4, H])
        msg = sb("msg", [P, 4, D + H])
        t_ps = [ps(f"t_ps{k}") for k in range(2)]
        q_ps = [ps(f"q_ps{k}") for k in range(2)]
        kv_ps = [ps(f"kv_ps{k}") for k in range(4)]
        spare_gp, index, src_in, dst_in = sem("spare_gp"), sem("index"), sems("src_in", 4), sems("dst_in", 4)
        turned, copied, q_done, kv_done, q_copied = sem("turned"), sem("copied"), sem("q_done"), sem("kv_done"), sem("q_copied")
        prodded, dotted, clipped, exped, scaled, stored = (sem("prodded"), sem("dotted"), sem("clipped"), sem("exped"),
                                                           sem("scaled"), sems("stored", 4))
        norm = float(C) ** 0.5
        win_out = sems("win_out", 8)
        x = a["x"]
        out_rows = by_column(msg0_d)

        with block() as blk:
            @blk.gpsimd
            def _(gp):
                def body(at):
                    c = at(0)
                    if not c:
                        return
                    r = ring(c, 4)
                    if had(c, 4):
                        gate(gp, spare_gp, turned, num(c) - 3)
                    gp.tensor_copy(cur[:, r, :], edge_rows[:, bass.ds(num(c), 1), :].rearrange("p c w -> p (c w)")).then_inc(index, 1)
                    gate(gp, spare_gp, index, num(c) + 1)
                    for k, arrived in enumerate((src_in, dst_in)):
                        gp.indirect_dma_start(out=xg[:, r, k, :], out_offset=None, in_=x,
                                              in_offset=bass.IndirectOffsetOnAxis(ap=cur[:, r, k:k + 1], axis=0))\
                          .then_inc(arrived[r], 16)
                run_steps(gp, EC, 0, body)

            @blk.tensor
            def _(pe):
                def body(at):
                    c = at(1)
                    if c:
                        r, b = ring(c, 4), ring(c, 2)
                        pe.wait_ge(src_in[r], turn(c, 4) * 16 + 16)
                        pe.wait_ge(dst_in[r], turn(c, 4) * 16 + 16)
                        if had(c, 2):
                            pe.wait_ge(copied, num(c) - 1)
                        for k in range(2):
                            for j in range(KC):
                                last = nc.tensor.transpose(t_ps[b][:, (k * KC + j) * P:(k * KC + j + 1) * P],
                                                           xg[:, r, k, j * P:(j + 1) * P], ident[:, :])
                        last.then_inc(turned, 1)
                    c = at(2)
                    if c:
                        r, b = ring(c, 4), ring(c, 2)
                        pe.wait_ge(copied, num(c) + 1)
                        if had(c, 2):
                            pe.wait_ge(q_copied, num(c) - 1)
                        for j in range(KC):
                            last = nc.tensor.matmul(q_ps[b][:, 0:D], xT[:, b, 1, j, :], w0_q[:, j, :], start=j == 0, stop=j == KC - 1)
                        last.then_inc(q_done, 1)
                        if had(c, 4):
                            pe.wait_ge(scaled, num(c) - 3)
                        for j in range(KC):
                            last = nc.tensor.matmul(kv_ps[r][:, :], xT[:, b, 0, j, :], w0_kv[:, j, :], start=j == 0, stop=j == KC - 1)
                        last.then_inc(kv_done, 1)
                run_steps(pe, EC, 2, body)

            @blk.scalar
            def _(act):
                def body(at):
                    c = at(1)
                    if c:
                        b = ring(c, 2)
                        act.wait_ge(turned, num(c) + 1)
                        if had(c, 2):
                            act.wait_ge(kv_done, num(c) - 1)
                        nc.scalar.activation(xT[:, b, :, :, :].rearrange("p k j e -> p (k j e)"), t_ps[b][:, :], ACT.Copy)\
                            .then_inc(copied, 1)
                    c = at(2)
                    if c:
                        b = ring(c, 2)
                        act.wait_ge(q_done, num(c) + 1)
                        if had(c, 2):
                            act.wait_ge(prodded, num(c) - 1)
                        nc.scalar.activation(qs[:, b, :], q_ps[b][:, 0:D], ACT.Copy).then_inc(q_copied, 1)
                    c = at(6)
                    if c:
                        act.wait_ge(scaled, num(c) + 1)
                        act.dma_start(out_rows[:, bass.ds(num(c), 1), :].rearrange("p c w -> p (c w)"), msg[:, ring(c, 4), :])\
                           .then_inc(stored[ring(c, 4)], 16)
                    c = at(4)
                    if c:
                        r = ring(c, 4)
                        act.wait_ge(clipped, num(c) + 1)
                        if had(c, 4):
                            act.wait_ge(stored[r], turn(c, 4) * 16)
                        nc.scalar.activation(msg[:, r, D:D + H], dots[:, r, :], ACT.Exp, scale=1.0 / norm).then_inc(exped, 1)
                run_steps(act, EC, 6, body)
                for k in range(4):
                    act.wait_ge(stored[k], 16 * (EC // 4))

            @blk.vector
            def _(ve):
                def body(at):
                    c = at(3)
                    if c:
                        ve.wait_ge(prodded, num(c) + 1)
                        nc.vector.tensor_reduce(dots[:, ring(c, 4), :], prod[:, ring(c, 2), :].rearrange("p (h c) -> p h c", h=H),
                                                axis=AX.X, op=ALU.add).then_inc(dotted, 1)
                    c = at(2)
                    if c:
                        r, b = ring(c, 4), ring(c, 2)
                        ve.wait_ge(kv_done, num(c) + 1)
                        ve.wait_ge(q_copied, num(c) + 1)
                        if had(c, 2):
                            ve.wait_ge(dotted, num(c) - 1)
                        nc.vector.tensor_tensor(prod[:, b, :], kv_ps[r][:, 0:D], qs[:, b, :], ALU.mult).then_inc(prodded, 1)
                    c = at(3)
                    if c:
                        ve.wait_ge(dotted, num(c) + 1)
                        nc.vector.tensor_scalar(dots[:, ring(c, 4), :], dots[:, ring(c, 4), :], -5.0 * norm, 5.0 * norm,
                                                ALU.max, ALU.min).then_inc(clipped, 1)
                    c = at(5)
                    if c:
                        r = ring(c, 4)
                        ve.wait_ge(exped, num(c) + 1)
                        nc.vector.tensor_tensor(msg[:, r, 0:D].rearrange("p (h c) -> p h c", h=H),
                                                kv_ps[r][:, D:2 * D].rearrange("p (h c) -> p h c", h=H),
                                                msg[:, r, D:D + H].unsqueeze(2).to_broadcast([P, H, C]), ALU.mult).then_inc(scaled, 1)
                run_steps(ve, EC, 5, body)

            @blk.sync
            def _(sp):
                def window(t):
                    if had(t, 8):
                        sp.wait_ge(win_out[ring(t, 8)], 16 * turn(t, 8))
                    first = sp.value_load(first_row[0:1, bass.ds(num(t), 1)], min_val=0, max_val=E)
                    sp.dma_start(windows[bass.ds(num(t), 1), :].rearrange("a (e w) -> a e w", w=2),
                                 edge_pairs[bass.ds(first, P), :].rearrange("(a e) w -> a e w", a=1))\
                      .then_inc(win_out[ring(t, 8)], 16)

                run_steps(sp, TILES, 0, lambda at: window(at(0)))
                for k in range(8):
                    sp.wait_ge(win_out[k], 16 * (TILES // 8))

    def turn_windows(sb, ps, sem, sems, block):
        wrow = sb("wrow", [WB, 4, 2 * P], I32)
        wrow_f = sb("wrow_f", [WB, 4, 2 * P])
        inside = sb("inside", [P, TILES])
        below = sb("below", [P, TILES])
        src_f = sb("src_f", [P, TILES])
        tr_ps, tr2_ps = ps("tr"), ps("tr2")
        win_in, cast, turned, d = sem("win_in"), sem("cast"), sem("turned"), sem("d")

        with block() as blk:
            @blk.sync
            def _(sp):
                sp.dma_start(wrow[:, :, :], windows.rearrange("(k t) w -> t k w", t=WB)).then_inc(win_in, 16)

            @blk.vector
            def _(ve):
                link = chained(ve, d)
                ve.wait_ge(win_in, 16)
                nc.vector.tensor_copy(wrow_f[:, :, :], wrow[:, :, :]).then_inc(cast, 1)
                ve.wait_ge(turned, 1)
                link(nc.vector.tensor_copy(src_f[:, :], tr_ps[:, 0:TILES]))
                ve.wait_ge(turned, 2)
                link(nc.vector.tensor_tensor(target_rel[:, :], tr2_ps[:, 0:TILES], tile_base[:, :], ALU.subtract))
                link(nc.vector.tensor_scalar(inside[:, :], target_rel[:, :], 0.0, None, ALU.is_ge))
                link(nc.vector.tensor_scalar(below[:, :], target_rel[:, :], float(P), None, ALU.is_lt))
                link(nc.vector.tensor_tensor(inside[:, :], inside[:, :], below[:, :], ALU.mult))
                link(nc.vector.tensor_scalar(inside[:, :], inside[:, :], -float(SKIP), float(SKIP), ALU.mult, ALU.add))
                link(nc.vector.tensor_tensor(source_row[:, :], src_f[:, :], inside[:, :], ALU.add))

            @blk.tensor
            def _(pe):
                pe.wait_ge(cast, 1)
                for w, t in enumerate((tr_ps, tr2_ps)):
                    for k in range(4):
                        last = nc.tensor.transpose(t[:, k * WB:(k + 1) * WB],
                                                   wrow_f[:, k, :].rearrange("p (e w) -> p e w", w=2)[:, :, w],
                                                   ident[0:WB, 0:WB])
                    last.then_inc(turned, 1)

    def one_hot(ve, u, hot, hot_ready, used, used_lag):
        b = ring(u, 2)
        if had(u, 2):
            ve.wait_ge(used, num(u) - 1 if used_lag is None else used_lag)
        rel = target_rel[:, bass.ds(num(u) * 2, 2)]
        nc.vector.tensor_tensor(hot[:, b, :, :], rel.unsqueeze(2).to_broadcast([P, 2, P]),
                                iota[:, :].unsqueeze(1).to_broadcast([P, 2, P]), ALU.is_equal).then_inc(hot_ready, 1)

    def norm_buffers(sb, sem, tag):
        t = {"rows": sb(tag + "_rows", [P, 4, 2, D]), "parts": sb(tag + "_parts", [P, 4, 2, 6]),
             "moments": sb(tag + "_moments", [P, 4, 2, 2])}
        for name in ("dev", "rstd", "shift"):
            t[name] = sb(f"{tag}_{name}", [P, 4, 2])
        for name in ("filled", "measured", "merged", "rooted", "inverted", "shifted", "normed"):
            t[name] = sem(f"{tag}_{name}")
        return t

    def norm_measure(ve, t, u):
        ve.wait_ge(t["filled"], num(u) + 1)
        for h in range(2):
            last = nc.vector.bn_stats(t["parts"][:, ring(u, 4), h, :], t["rows"][:, ring(u, 4), h, :])
        last.then_inc(t["measured"], 1)

    def norm_merge(ve, t, u, spare):
        gate(ve, spare, t["measured"], num(u) + 1)
        for h in range(2):
            last = nc.vector.bn_aggr(t["moments"][:, ring(u, 4), h, :], t["parts"][:, ring(u, 4), h, :])
        last.then_inc(t["merged"], 1)

    def norm_root(act, t, u):
        act.wait_ge(t["merged"], num(u) + 1)
        nc.scalar.activation(t["dev"][:, ring(u, 4), :], t["moments"][:, ring(u, 4), :, 1], ACT.Sqrt,
                             bias=eps_ln[:, :]).then_inc(t["rooted"], 1)

    def norm_invert(ve, t, u):
        ve.wait_ge(t["rooted"], num(u) + 1)
        nc.vector.reciprocal(t["rstd"][:, ring(u, 4), :], t["dev"][:, ring(u, 4), :]).then_inc(t["inverted"], 1)

    def norm_shift(ve, t, u):
        ve.wait_ge(t["inverted"], num(u) + 1)
        nc.vector.scalar_tensor_tensor(t["shift"][:, ring(u, 4), :], t["moments"][:, ring(u, 4), :, 0], -1.0,
                                       t["rstd"][:, ring(u, 4), :], ALU.mult, ALU.mult).then_inc(t["shifted"], 1)

    def norm_apply(act, t, u, to):
        act.wait_ge(t["shifted"], num(u) + 1)
        for h in range(2):
            last = nc.scalar.activation(to[:, h, :], t["rows"][:, ring(u, 4), h, :], ACT.Identity,
                                        bias=t["shift"][:, ring(u, 4), h:h + 1], scale=t["rstd"][:, ring(u, 4), h:h + 1])
        last.then_inc(t["normed"], 1)

    def load_unit(sp, u, to, table, arrived, rows_of_last=P):
        if rows_of_last < P and is_last(u, UNITS):
            sp.dma_start(to[0:rows_of_last, 0, :], table[(TILES - 2) * P:N, :]).then_inc(arrived, 16)
        else:
            full = UNITS - (rows_of_last < P)
            sp.dma_start(to, by_unit(table[0:full * 2 * P, :])[:, bass.ds(num(u), 1), :, :].rearrange("p u h w -> p (u h) w"))\
              .then_inc(arrived, 16)

    def load_windows(sp, u, pairs):
        for h in range(2):
            first = sp.value_load(first_row[0:1, bass.ds(num(u) * 2 + h, 1)], min_val=0, max_val=E)
            for table, to, arrived in pairs:
                sp.dma_start(to[:, h, :], table[bass.ds(first, P), :]).then_inc(arrived[h], 16)

    def by_head(t):
        return t.rearrange("p u (h c) -> p u h c", h=H)

    def over_head(t):
        return t.unsqueeze(3).to_broadcast([P, 2, H, C])

    def both(row):
        return row[:, :].unsqueeze(1).to_broadcast([P, 2, D])

    def nodes0(sb, ps, sem, sems, block):
        xin = sb("xin", [P, 4, 2, D])
        msg = sb("msg", [P, 4, 2, D + H])
        hot = sb("hot", [P, 2, 2, P])
        den = sb("den", [P, 2, 2, H])
        mean_msg = sb("mean_msg", [P, 2, 2, D])
        y = sb("y", [P, 4, 2, D])
        ln = norm_buffers(sb, sem, "ln")
        agg = [ps(f"agg{k}", 2) for k in range(2)]
        x_in, msg_in, stored = sems("x_in", 4), [sems(f"msg_in{k}", 2) for k in range(4)], sems("stored", 4)
        hot_ready, summed, eps_added, inverse, divided, spare_ve = (sem("hot_ready"), sem("summed"), sem("eps_added"),
                                                                    sem("inverse"), sem("divided"), sem("spare_ve"))

        with block() as blk:
            @blk.sync
            def _(sp):
                def body(at):
                    u = at(0)
                    r = ring(u, 4)
                    if had(u, 4):
                        sp.wait_ge(ln["filled"], num(u) - 3)
                        sp.wait_ge(summed, num(u) - 3)
                    load_unit(sp, u, xin[:, r, :, :], a["x"], x_in[r], LAST_ROWS)
                    load_windows(sp, u, [(msg0_d, msg[:, r, :, :], msg_in[r])])
                run_steps(sp, UNITS, 0, body)

            @blk.vector
            def _(ve):
                def body(at):
                    u = at(4)
                    if u:
                        norm_invert(ve, ln, u)
                    u = at(2)
                    if u:
                        ve.wait_ge(summed, num(u) + 1)
                        z = agg[ring(u, 2)][:, :, D:D + H]
                        nc.vector.tensor_scalar(den[:, ring(u, 2), :, :], z, 1e-9, None, ALU.add).then_inc(eps_added, 1)
                    u = at(0)
                    if u:
                        one_hot(ve, u, hot, hot_ready, summed, None)
                    u = at(2)
                    if u:
                        ve.wait_ge(eps_added, num(u) + 1)
                        nc.vector.reciprocal(den[:, ring(u, 2), :, :], den[:, ring(u, 2), :, :]).then_inc(inverse, 1)
                    u = at(3)
                    if u:
                        norm_measure(ve, ln, u)
                    u = at(4)
                    if u:
                        norm_shift(ve, ln, u)
                    u = at(2)
                    if u:
                        ve.wait_ge(inverse, num(u) + 1)
                        nc.vector.tensor_tensor(by_head(mean_msg[:, ring(u, 2), :, :]), by_head(agg[ring(u, 2)][:, :, 0:D]),
                                                over_head(den[:, ring(u, 2), :, :]), ALU.mult).then_inc(divided, 1)
                    u = at(3)
                    if u:
                        norm_merge(ve, ln, u, spare_ve)
                    u = at(2)
                    if u:
                        ve.wait_ge(divided, num(u) + 1)
                        ve.wait_ge(x_in[ring(u, 4)], turn(u, 4) * 16 + 16)
                        if had(u, 4):
                            ve.wait_ge(ln["normed"], num(u) - 3)
                        nc.vector.tensor_tensor(ln["rows"][:, ring(u, 4), :, :], mean_msg[:, ring(u, 2), :, :], xin[:, ring(u, 4), :, :], ALU.add)\
                            .then_inc(ln["filled"], 1)
                run_steps(ve, UNITS, 4, body)

            @blk.tensor
            def _(pe):
                def body(at):
                    u = at(1)
                    if not u:
                        return
                    r = ring(u, 4)
                    pe.wait_ge(hot_ready, num(u) + 1)
                    if had(u, 2):
                        pe.wait_ge(divided, num(u) - 1)
                    for h in range(2):
                        pe.wait_ge(msg_in[r][h], turn(u, 4) * 16 + 16)
                        last = nc.tensor.matmul(agg[ring(u, 2)][:, h, 0:D + H], hot[:, ring(u, 2), h, :], msg[:, r, h, :],
                                                start=True, stop=True)
                    last.then_inc(summed, 1)
                run_steps(pe, UNITS, 1, body)

            @blk.scalar
            def _(act):
                def body(at):
                    u = at(3)
                    if u:
                        norm_root(act, ln, u)
                    u = at(4)
                    if u:
                        if had(u, 4):
                            act.wait_ge(stored[ring(u, 4)], turn(u, 4) * 16)
                        norm_apply(act, ln, u, y[:, ring(u, 4), :, :])
                    u = at(5)
                    if u:
                        act.wait_ge(ln["normed"], num(u) + 1)
                        act.dma_start(by_unit(x1_d)[:, bass.ds(num(u), 1), :, :].rearrange("p u h w -> p (u h) w"), y[:, ring(u, 4), :, :])\
                           .then_inc(stored[ring(u, 4)], 16)
                run_steps(act, UNITS, 5, body)
                for k in range(4):
                    act.wait_ge(stored[k], 16 * (UNITS // 4))

    def nodes1(sb, ps, sem, sems, block):
        xin = sb("xin", [P, 8, 2, D])
        cur = sb("cur", [P, 4, 2], I32)
        near_rows = sb("near_rows", [P, 4, 2, D])
        xb = sb("xb", [P, 4, 2, D])
        hot = sb("hot", [P, 2, 2, P])
        z = sb("z", [P, 2, 2, D])
        zT = sb("zT", [P, 2, KC, 2, P])
        hid = sb("hid", [P, 2, KC, 2 * P])
        scaled = sb("scaled", [P, 2, 2, D])
        affine = sb("affine", [P, 2, 2, D])
        x2 = sb("x2", [P, 4, 2, D])
        x2T = sb("x2T", [P, 2, KC, 2, P])
        hh = sb("hh", [P, 4, 2, D + 2 * H])
        inner = norm_buffers(sb, sem, "inner")
        outer = norm_buffers(sb, sem, "outer")
        agg_ps, zT_ps, hid_ps, xT_ps, h_ps = ps("agg"), ps("zT_ps"), ps("hid_ps"), ps("xT_ps"), ps("h_ps", 2)
        out_ps = [ps(f"out_ps{k}") for k in range(2)]
        x_in, near_in, x2_out, h_out, att_out = (sems("x_in", 8), [sems(f"near_in{k}", 2) for k in range(4)], sems("x2_out", 4),
                                                 sems("h_out", 4), sems("att_out", 4))
        zeroed, index, spare_gp, spare_ve, biased = sem("zeroed"), sem("index"), sem("spare_gp"), sem("spare_ve"), sem("biased")
        hot_ready, summed, added, z_turned, z_copied = (sem("hot_ready"), sem("summed"), sem("added"), sem("z_turned"), sem("z_copied"))
        hid_done, hid_relu, out_done, gamma_done, beta_done = (sem("hid_done"), sem("hid_relu"), sem("out_done"),
                                                               sem("gamma_done"), sem("beta_done"))
        x_turned, x_copied, h_done, h_copied = sem("x_turned"), sem("x_copied"), sem("h_done"), sem("h_copied")

        with block() as blk:
            @blk.sync
            def _(sp):
                def body(at):
                    u = at(0)
                    if u:
                        if had(u, 8):
                            sp.wait_ge(outer["filled"], num(u) - 7)
                        load_unit(sp, u, xin[:, ring(u, 8), :, :], x1_d, x_in[ring(u, 8)])
                run_steps(sp, UNITS, 0, body)

            @blk.gpsimd
            def _(gp):
                gp.memset(near_rows[:, :, :, :], 0.0).then_inc(zeroed, 1)

                def body(at):
                    u = at(0)
                    if u:
                        r = ring(u, 4)
                        if had(u, 4):
                            gate(gp, spare_gp, summed, num(u) - 3)
                        gp.tensor_copy(cur[:, r, :], source_row[:, bass.ds(num(u) * 2, 2)]).then_inc(index, 1)
                        gate(gp, spare_gp, index, num(u) + 1)
                        if not had(u, 1):
                            gp.wait_ge(zeroed, 1)
                        for h in range(2):
                            gp.indirect_dma_start(out=near_rows[:, r, h, :], out_offset=None, in_=x1_d,
                                                  in_offset=bass.IndirectOffsetOnAxis(ap=cur[:, r, h:h + 1], axis=0),
                                                  bounds_check=NPAD - 1, oob_is_err=False).then_inc(near_in[r][h], 16)
                    u = at(2)
                    if u:
                        gp.wait_ge(x_in[ring(u, 8)], turn(u, 8) * 16 + 16)
                        if had(u, 4):
                            gp.wait_ge(inner["filled"], num(u) - 3)
                        gp.tensor_tensor(xb[:, ring(u, 4), :, :], xin[:, ring(u, 8), :, :], both(rows["L1_gnn_b2"]), ALU.add)\
                          .then_inc(biased, 1)
                run_steps(gp, UNITS, 2, body)

            @blk.vector
            def _(ve):
                def body(at):
                    u = at(2)
                    if u:
                        ve.wait_ge(x_in[ring(u, 8)], turn(u, 8) * 16 + 16)
                        ve.wait_ge(summed, num(u) + 1)
                        if had(u, 2):
                            ve.wait_ge(z_turned, num(u) - 1)
                        nc.vector.scalar_tensor_tensor(z[:, ring(u, 2), :, :], xin[:, ring(u, 8), :, :], gin[:, 0:1],
                                                       agg_ps[:, :].rearrange("p (h w) -> p h w", h=2), ALU.mult, ALU.add)\
                            .then_inc(added, 1)
                    u = at(0)
                    if u:
                        one_hot(ve, u, hot, hot_ready, summed, None)
                    u = at(5)
                    if u:
                        ve.wait_ge(out_done, num(u) + 1)
                        ve.wait_ge(biased, num(u) + 1)
                        if had(u, 4):
                            ve.wait_ge(gamma_done, num(u) - 3)
                        nc.vector.tensor_tensor(inner["rows"][:, ring(u, 4), :, :], out_ps[ring(u, 2)][:, :].rearrange("p (h w) -> p h w", h=2),
                                                xb[:, ring(u, 4), :, :], ALU.add).then_inc(inner["filled"], 1)
                    u = at(6)
                    if u:
                        norm_measure(ve, inner, u)
                    u = at(8)
                    if u:
                        norm_measure(ve, outer, u)
                    u = at(7)
                    if u:
                        ve.wait_ge(inner["merged"], num(u) + 1)
                        b = ring(u, 2)
                        if had(u, 2):
                            ve.wait_ge(beta_done, num(u) - 1)
                        for h in range(2):
                            last = nc.vector.scalar_tensor_tensor(scaled[:, b, h, :], inner["rows"][:, ring(u, 4), h, :],
                                                                  inner["moments"][:, ring(u, 4), h, 0:1], rows["L1_gnn_gamma"][:, :],
                                                                  ALU.subtract, ALU.mult)
                        last.then_inc(gamma_done, 1)
                    u = at(7)
                    if u:
                        norm_invert(ve, inner, u)
                    u = at(9)
                    if u:
                        norm_invert(ve, outer, u)
                    u = at(6)
                    if u:
                        norm_merge(ve, inner, u, spare_ve)
                    u = at(8)
                    if u:
                        norm_merge(ve, outer, u, spare_ve)
                    u = at(7)
                    if u:
                        ve.wait_ge(gamma_done, num(u) + 1)
                        ve.wait_ge(inner["inverted"], num(u) + 1)
                        if had(u, 2):
                            ve.wait_ge(outer["filled"], num(u) - 1)
                        for h in range(2):
                            last = nc.vector.scalar_tensor_tensor(affine[:, ring(u, 2), h, :], scaled[:, ring(u, 2), h, :],
                                                                  inner["rstd"][:, ring(u, 4), h:h + 1], rows["L1_gnn_beta"][:, :],
                                                                  ALU.mult, ALU.add)
                        last.then_inc(beta_done, 1)
                    u = at(9)
                    if u:
                        norm_shift(ve, outer, u)
                    u = at(7)
                    if u:
                        ve.wait_ge(beta_done, num(u) + 1)
                        if had(u, 4):
                            ve.wait_ge(outer["normed"], num(u) - 3)
                        nc.vector.scalar_tensor_tensor(outer["rows"][:, ring(u, 4), :, :], affine[:, ring(u, 2), :, :], 0.0, xin[:, ring(u, 8), :, :],
                                                       ALU.max, ALU.add).then_inc(outer["filled"], 1)
                run_steps(ve, UNITS, 9, body)

            @blk.tensor
            def _(pe):
                pe.wait_ge(zeroed, 1)

                def body(at):
                    u = at(4)
                    if u:
                        pe.wait_ge(hid_relu, num(u) + 1)
                        if had(u, 2):
                            pe.wait_ge(inner["filled"], num(u) - 1)
                        for h in range(2):
                            for k in range(KC):
                                last = nc.tensor.matmul(out_ps[ring(u, 2)][:, h * D:(h + 1) * D], hid[:, ring(u, 2), k, h * P:(h + 1) * P],
                                                        w1_b[:, k, :], start=k == 0, stop=k == KC - 1)
                        last.then_inc(out_done, 1)
                    u = at(12)
                    if u:
                        pe.wait_ge(x_copied, num(u) + 1)
                        if had(u, 1):
                            pe.wait_ge(h_copied, num(u))
                        for h in range(2):
                            for k in range(KC):
                                last = nc.tensor.matmul(h_ps[:, h, 0:D + 2 * H], x2T[:, ring(u, 2), k, h, :], w2_h[:, k, :],
                                                        start=k == 0, stop=k == KC - 1)
                        last.then_inc(h_done, 1)
                    u = at(3)
                    if u:
                        pe.wait_ge(z_copied, num(u) + 1)
                        if had(u, 1):
                            pe.wait_ge(hid_relu, num(u))
                        for m in range(KC):
                            for k in range(KC):
                                last = nc.tensor.matmul(hid_ps[:, m * 2 * P:(m + 1) * 2 * P], w1_a[:, k, m * P:(m + 1) * P],
                                                        zT[:, ring(u, 2), k, :, :].rearrange("p h n -> p (h n)"),
                                                        start=k == 0, stop=k == KC - 1)
                        last.then_inc(hid_done, 1)
                    u = at(1)
                    if u:
                        r = ring(u, 4)
                        pe.wait_ge(hot_ready, num(u) + 1)
                        if had(u, 1):
                            pe.wait_ge(added, num(u))
                        for h in range(2):
                            pe.wait_ge(near_in[r][h], turn(u, 4) * 16 + 16)
                            last = nc.tensor.matmul(agg_ps[:, h * D:(h + 1) * D], hot[:, ring(u, 2), h, :], near_rows[:, r, h, :],
                                                    start=True, stop=True)
                        last.then_inc(summed, 1)
                    u = at(11)
                    if u:
                        pe.wait_ge(outer["normed"], num(u) + 1)
                        if had(u, 1):
                            pe.wait_ge(x_copied, num(u))
                        for k in range(KC):
                            for h in range(2):
                                last = nc.tensor.transpose(xT_ps[:, (k * 2 + h) * P:(k * 2 + h + 1) * P],
                                                           x2[:, ring(u, 4), h, k * P:(k + 1) * P], ident[:, :])
                        last.then_inc(x_turned, 1)
                    u = at(2)
                    if u:
                        pe.wait_ge(added, num(u) + 1)
                        if had(u, 1):
                            pe.wait_ge(z_copied, num(u))
                        for k in range(KC):
                            for h in range(2):
                                last = nc.tensor.transpose(zT_ps[:, (k * 2 + h) * P:(k * 2 + h + 1) * P],
                                                           z[:, ring(u, 2), h, k * P:(k + 1) * P], ident[:, :])
                        last.then_inc(z_turned, 1)
                run_steps(pe, UNITS, 12, body)

            @blk.scalar
            def _(act):
                def body(at):
                    u = at(10)
                    if u:
                        if had(u, 4):
                            act.wait_ge(x2_out[ring(u, 4)], turn(u, 4) * 16)
                            act.wait_ge(x_turned, num(u) - 3)
                        norm_apply(act, outer, u, x2[:, ring(u, 4), :, :])
                    u = at(12)
                    if u:
                        act.wait_ge(h_done, num(u) + 1)
                        if had(u, 4):
                            act.wait_ge(h_out[ring(u, 4)], turn(u, 4) * 16)
                            act.wait_ge(att_out[ring(u, 4)], turn(u, 4) * 16)
                        nc.scalar.activation(hh[:, ring(u, 4), :, :], h_ps[:, :, 0:D + 2 * H], ACT.Copy).then_inc(h_copied, 1)
                    u = at(3)
                    if u:
                        act.wait_ge(hid_done, num(u) + 1)
                        if had(u, 2):
                            act.wait_ge(out_done, num(u) - 1)
                        for m in range(KC):
                            last = nc.scalar.activation(hid[:, ring(u, 2), m, :], hid_ps[:, m * 2 * P:(m + 1) * 2 * P], ACT.Relu,
                                                        bias=b1[:, m:m + 1])
                        last.then_inc(hid_relu, 1)
                    u = at(11)
                    if u:
                        act.wait_ge(x_turned, num(u) + 1)
                        if had(u, 2):
                            act.wait_ge(h_done, num(u) - 1)
                        nc.scalar.activation(x2T[:, ring(u, 2), :, :, :].rearrange("p k h n -> p (k h n)"), xT_ps[:, :], ACT.Copy)\
                            .then_inc(x_copied, 1)
                        act.wait_ge(outer["normed"], num(u) + 1)
                        act.dma_start(unit_rows(x2_d, u), x2[:, ring(u, 4), :, :]).then_inc(x2_out[ring(u, 4)], 16)
                    u = at(2)
                    if u:
                        act.wait_ge(z_turned, num(u) + 1)
                        if had(u, 2):
                            act.wait_ge(hid_done, num(u) - 1)
                        nc.scalar.activation(zT[:, ring(u, 2), :, :, :].rearrange("p k h n -> p (k h n)"), zT_ps[:, :], ACT.Copy)\
                            .then_inc(z_copied, 1)
                    u = at(6)
                    if u:
                        norm_root(act, inner, u)
                    u = at(8)
                    if u:
                        norm_root(act, outer, u)
                    u = at(13)
                    if u:
                        act.wait_ge(h_copied, num(u) + 1)
                        act.dma_start(unit_rows(h_d, u), hh[:, ring(u, 4), :, 0:D]).then_inc(h_out[ring(u, 4)], 16)
                        act.dma_start(unit_rows(att_d, u), hh[:, ring(u, 4), :, D:D + 2 * H]).then_inc(att_out[ring(u, 4)], 16)
                run_steps(act, UNITS, 13, body)
                for k in range(4):
                    for s in (x2_out, h_out, att_out):
                        act.wait_ge(s[k], 16 * (UNITS // 4))

    def unit_rows(table, u):
        return by_unit(table)[:, bass.ds(num(u), 1), :, :].rearrange("p u h w -> p (u h) w")

    def shares(sb, ps, sem, sems, block, self_scores, shares_d, width):
        top_score = sb("top_score", [P, EC, H])
        work = sb("work", [P, EC, H])
        share = sb("share", [P, EC, width])
        end, carry = sb("end", [P, H]), sb("carry", [P, H])
        chain, shifted = sb("chain", [H, P]), sb("chain_shifted", [H, P])
        turn_ps, back_ps = ps("turn_ps"), ps("back_ps")
        d, end_ready, end_turned, chain_ready, chain_turned = (sem("d"), sem("end_ready"), sem("end_turned"), sem("chain_ready"),
                                                               sem("chain_turned"))
        less_top, exped, out_sem = sem("less_top"), sem("exped"), sem("shares_out")
        scans = 4

        with block() as blk:
            @blk.vector
            def _(ve):
                link = chained(ve, d)
                done = [0]

                def scan(to, what, joins, joins_chain, op0, op1, start, back):
                    step = -1 if back else 1
                    first, last = (EC - 1, 0) if back else (0, EC - 1)
                    for again in range(2):
                        for h in range(H):
                            link(nc.vector.tensor_tensor_scan(to[:, ::step, h], joins[:, ::step], what[:, ::step, h],
                                                              carry[:, h:h + 1] if again else start, op0, op1))
                        if again:
                            break
                        done[0] += 1
                        nc.vector.tensor_copy(end[:, :], to[:, last, :]).then_inc(end_ready, 1)
                        ve.wait_ge(end_turned, done[0])
                        link(nc.vector.tensor_tensor_scan(chain[:, ::step], joins_chain[:, ::step], turn_ps[0:H, 0:P][:, ::step],
                                                          start, op0, op1))
                        link(nc.vector.memset(shifted[:, :], start))
                        if back:
                            nc.vector.tensor_copy(shifted[:, 0:P - 1], chain[:, 1:P]).then_inc(chain_ready, 1)
                        else:
                            nc.vector.tensor_copy(shifted[:, 1:P], chain[:, 0:P - 1]).then_inc(chain_ready, 1)
                        ve.wait_ge(chain_turned, done[0])
                        link(nc.vector.tensor_copy(carry[:, :], back_ps[:, 0:H]))

                def tt(to, x, y, op):
                    return nc.vector.tensor_tensor(to, x, y, op)

                scan(work, scores, join_prev, chain_max, ALU.add, ALU.max, -BIG, False)
                scan(top_score, work, join_next, chain_next, ALU.add, ALU.max, -BIG, True)
                if self_scores is not None:
                    link(tt(top_score[:, :, :], top_score[:, :, :], self_scores[:, :, :], ALU.max))
                    link(tt(self_scores[:, :, :], self_scores[:, :, :], top_score[:, :, :], ALU.subtract))
                tt(scores[:, :, :], scores[:, :, :], top_score[:, :, :], ALU.subtract).then_inc(less_top, 1)
                ve.wait_ge(exped, 1)
                scan(work, scores, keep_prev, chain_sum, ALU.mult, ALU.add, 0.0, False)
                scan(top_score, work, join_next, chain_next, ALU.add, ALU.max, -BIG, True)
                if self_scores is not None:
                    link(tt(top_score[:, :, :], top_score[:, :, :], self_scores[:, :, :], ALU.add))
                link(nc.vector.reciprocal(top_score[:, :, :], top_score[:, :, :]))
                if self_scores is not None:
                    link(tt(self_scores[:, :, :], self_scores[:, :, :], top_score[:, :, :], ALU.mult))
                    link(nc.vector.scalar_tensor_tensor(share[:, :, H:2 * H], self_scores[:, :, :], -1.0,
                                                        first_mark[:, :].unsqueeze(2).to_broadcast([P, EC, H]), ALU.add, ALU.mult))
                link(tt(share[:, :, 0:H], scores[:, :, :], top_score[:, :, :], ALU.mult))

            @blk.tensor
            def _(pe):
                for n in range(scans):
                    pe.wait_ge(end_ready, n + 1)
                    nc.tensor.transpose(turn_ps[0:H, 0:P], end[:, :], ident[:, :]).then_inc(end_turned, 1)
                    pe.wait_ge(chain_ready, n + 1)
                    nc.tensor.transpose(back_ps[:, 0:H], shifted[:, :], ident[0:H, 0:H]).then_inc(chain_turned, 1)

            @blk.scalar
            def _(act):
                act.wait_ge(less_top, 1)
                if self_scores is not None:
                    nc.scalar.activation(self_scores[:, :, :], self_scores[:, :, :], ACT.Exp)
                nc.scalar.activation(scores[:, :, :], scores[:, :, :], ACT.Exp).then_inc(exped, 1)

            @blk.sync
            def _(sp):
                per_scan = 2 * H + 3
                sp.wait_ge(d, scans * per_scan + 2 + (5 if self_scores is not None else 0))
                sp.dma_start(shares_d[0:EPAD, :].rearrange("(p c) w -> p (c w)", c=EC),
                             share[:, :, :].rearrange("p c w -> p (c w)")).then_inc(out_sem, 16)
                sp.wait_ge(out_sem, 16)

    def edges2(sb, ps, sem, sems, block, self_scores):
        cur = sb("cur", [P, 4, 2], I32)
        terms = sb("terms", [P, 4, 2, 2 * H])
        both_sums = sb("both_sums", [P, 4, 2, H])
        spare_gp, index, src_in, dst_in = sem("spare_gp"), sem("index"), sems("src_in", 4), sems("dst_in", 4)
        summed, placed = sem("summed"), sem("placed")

        with block() as blk:
            @blk.gpsimd
            def _(gp):
                def body(at):
                    c = at(0)
                    r = ring(c, 4)
                    if had(c, 4):
                        gate(gp, spare_gp, summed, num(c) - 3)
                    gp.tensor_copy(cur[:, r, :], edge_rows[:, bass.ds(num(c), 1), :].rearrange("p c w -> p (c w)")).then_inc(index, 1)
                    gate(gp, spare_gp, index, num(c) + 1)
                    for k, arrived in enumerate((src_in, dst_in)):
                        gp.indirect_dma_start(out=terms[:, r, k, :], out_offset=None, in_=att_d,
                                              in_offset=bass.IndirectOffsetOnAxis(ap=cur[:, r, k:k + 1], axis=0))\
                          .then_inc(arrived[r], 16)
                run_steps(gp, EC, 0, body)

            @blk.vector
            def _(ve):
                def body(at):
                    c = at(0)
                    if c:
                        r = ring(c, 4)
                        ve.wait_ge(src_in[r], turn(c, 4) * 16 + 16)
                        ve.wait_ge(dst_in[r], turn(c, 4) * 16 + 16)
                        if had(c, 4):
                            ve.wait_ge(placed, num(c) - 3)
                        nc.vector.tensor_tensor(both_sums[:, r, :, :], terms[:, r, :, 0:H],
                                                terms[:, r, 1, H:2 * H].unsqueeze(1).to_broadcast([P, 2, H]), ALU.add)\
                            .then_inc(summed, 1)
                    c = at(1)
                    if c:
                        ve.wait_ge(summed, num(c) + 1)
                        for k, to in enumerate((scores, self_scores)):
                            t = both_sums[:, ring(c, 4), k, :]
                            last = nc.vector.scalar_tensor_tensor(to[:, bass.ds(num(c), 1), :].rearrange("p c w -> p (c w)"),
                                                                  t, 0.2, t, ALU.mult, ALU.max)
                        last.then_inc(placed, 1)
                run_steps(ve, EC, 1, body)

    def nodes2(sb, ps, sem, sems, block):
        xin = sb("xin", [P, 8, 2, D])
        hin = sb("hin", [P, 4, 2, D])
        part = sb("part", [P, 4, 2, 2 * H])
        cur = sb("cur", [P, 4, 2], I32)
        near_rows = sb("near_rows", [P, 4, 2, D])
        xb = sb("xb", [P, 4, 2, D])
        hot = sb("hot", [P, 2, 2, P])
        weighted = sb("weighted", [P, 2, 2, D])
        own_share = sb("own_share", [P, 4, 2, H])
        own = sb("own", [P, 4, 2, D])
        gat = sb("gat", [P, 2, 2, D])
        scaled = sb("scaled", [P, 2, 2, D])
        affine = sb("affine", [P, 2, 2, D])
        x3 = sb("x3", [P, 4, 2, D])
        inner = norm_buffers(sb, sem, "inner")
        outer = norm_buffers(sb, sem, "outer")
        agg = [ps(f"agg{k}", 2) for k in range(4)]
        x_in, h_in, near_in, part_in, stored = (sems("x_in", 8), sems("h_in", 4), [sems(f"near_in{k}", 2) for k in range(4)],
                                                [sems(f"part_in{k}", 2) for k in range(4)], sems("stored", 4))
        zeroed, index, spare_gp, spare_ve, biased, own_done = (sem("zeroed"), sem("index"), sem("spare_gp"), sem("spare_ve"),
                                                               sem("biased"), sem("own_done"))
        hot_ready, weighed, summed, own_known, gat_done, gamma_done, beta_done = (
            sem("hot_ready"), sem("weighed"), sem("summed"), sem("own_known"), sem("gat_done"), sem("gamma_done"), sem("beta_done"))

        with block() as blk:
            @blk.sync
            def _(sp):
                def body(at):
                    u = at(0)
                    r = ring(u, 4)
                    if had(u, 8):
                        sp.wait_ge(outer["filled"], num(u) - 7)
                    load_unit(sp, u, xin[:, ring(u, 8), :, :], x2_d, x_in[ring(u, 8)])
                    if had(u, 4):
                        sp.wait_ge(own_done, num(u) - 3)
                        sp.wait_ge(summed, num(u) - 3)
                    load_unit(sp, u, hin[:, r, :, :], h_d, h_in[r])
                    load_windows(sp, u, [(share2_d, part[:, r, :, :], part_in[r])])
                run_steps(sp, UNITS, 0, body)

            @blk.gpsimd
            def _(gp):
                gp.memset(near_rows[:, :, :, :], 0.0).then_inc(zeroed, 1)

                def body(at):
                    u = at(0)
                    if u:
                        r = ring(u, 4)
                        if had(u, 4):
                            gate(gp, spare_gp, weighed, num(u) - 3)
                        gp.tensor_copy(cur[:, r, :], source_row[:, bass.ds(num(u) * 2, 2)]).then_inc(index, 1)
                        gate(gp, spare_gp, index, num(u) + 1)
                        if not had(u, 1):
                            gp.wait_ge(zeroed, 1)
                        for h in range(2):
                            gp.indirect_dma_start(out=near_rows[:, r, h, :], out_offset=None, in_=h_d,
                                                  in_offset=bass.IndirectOffsetOnAxis(ap=cur[:, r, h:h + 1], axis=0),
                                                  bounds_check=NPAD - 1, oob_is_err=False).then_inc(near_in[r][h], 16)
                    u = at(1)
                    if u:
                        gp.wait_ge(x_in[ring(u, 8)], turn(u, 8) * 16 + 16)
                        if had(u, 4):
                            gp.wait_ge(inner["filled"], num(u) - 3)
                        gp.tensor_tensor(xb[:, ring(u, 4), :, :], xin[:, ring(u, 8), :, :], both(rows["L2_gnn_bias"]), ALU.add)\
                          .then_inc(biased, 1)
                    u = at(3)
                    if u:
                        gp.wait_ge(own_known, num(u) + 1)
                        gp.wait_ge(h_in[ring(u, 4)], turn(u, 4) * 16 + 16)
                        if had(u, 4):
                            gp.wait_ge(gat_done, num(u) - 3)
                        gp.tensor_tensor(by_head(own[:, ring(u, 4), :, :]), by_head(hin[:, ring(u, 4), :, :]),
                                         over_head(own_share[:, ring(u, 4), :, :]), ALU.mult).then_inc(own_done, 1)
                run_steps(gp, UNITS, 3, body)

            @blk.vector
            def _(ve):
                ve.wait_ge(zeroed, 1)

                def body(at):
                    u = at(5)
                    if u:
                        norm_invert(ve, inner, u)
                    u = at(7)
                    if u:
                        norm_invert(ve, outer, u)
                    u = at(0)
                    if u:
                        one_hot(ve, u, hot, hot_ready, summed, None)
                    u = at(7)
                    if u:
                        norm_shift(ve, outer, u)
                    u = at(2)
                    if u:
                        ve.wait_ge(summed, num(u) + 1)
                        if had(u, 4):
                            ve.wait_ge(own_done, num(u) - 3)
                        nc.vector.tensor_scalar(own_share[:, ring(u, 4), :, :], agg[ring(u, 4)][:, :, D:D + H], 1.0, None, ALU.add)\
                            .then_inc(own_known, 1)
                    u = at(5)
                    if u:
                        ve.wait_ge(inner["merged"], num(u) + 1)
                        if had(u, 2):
                            ve.wait_ge(beta_done, num(u) - 1)
                        for h in range(2):
                            last = nc.vector.scalar_tensor_tensor(scaled[:, ring(u, 2), h, :], inner["rows"][:, ring(u, 4), h, :],
                                                                  inner["moments"][:, ring(u, 4), h, 0:1], rows["L2_gnn_ln_w"][:, :],
                                                                  ALU.subtract, ALU.mult)
                        last.then_inc(gamma_done, 1)
                    u = at(0)
                    if u:
                        r = ring(u, 4)
                        for h in range(2):
                            ve.wait_ge(near_in[r][h], turn(u, 4) * 16 + 16)
                            ve.wait_ge(part_in[r][h], turn(u, 4) * 16 + 16)
                        if had(u, 2):
                            ve.wait_ge(summed, num(u) - 1)
                        nc.vector.tensor_tensor(by_head(weighted[:, ring(u, 2), :, :]), by_head(near_rows[:, r, :, :]),
                                                over_head(part[:, r, :, 0:H]), ALU.mult).then_inc(weighed, 1)
                    u = at(4)
                    if u:
                        norm_measure(ve, inner, u)
                    u = at(5)
                    if u:
                        ve.wait_ge(gamma_done, num(u) + 1)
                        ve.wait_ge(inner["inverted"], num(u) + 1)
                        if had(u, 2):
                            ve.wait_ge(outer["filled"], num(u) - 1)
                        for h in range(2):
                            last = nc.vector.scalar_tensor_tensor(affine[:, ring(u, 2), h, :], scaled[:, ring(u, 2), h, :],
                                                                  inner["rstd"][:, ring(u, 4), h:h + 1], rows["L2_gnn_ln_b"][:, :],
                                                                  ALU.mult, ALU.add)
                        last.then_inc(beta_done, 1)
                    u = at(3)
                    if u:
                        ve.wait_ge(own_done, num(u) + 1)
                        if had(u, 2):
                            ve.wait_ge(inner["filled"], num(u) - 1)
                        nc.vector.tensor_tensor(gat[:, ring(u, 2), :, :], agg[ring(u, 4)][:, :, 0:D], own[:, ring(u, 4), :, :], ALU.add)\
                            .then_inc(gat_done, 1)
                    u = at(4)
                    if u:
                        norm_merge(ve, inner, u, spare_ve)
                    u = at(6)
                    if u:
                        norm_measure(ve, outer, u)
                    u = at(3)
                    if u:
                        ve.wait_ge(gat_done, num(u) + 1)
                        ve.wait_ge(biased, num(u) + 1)
                        if had(u, 4):
                            ve.wait_ge(gamma_done, num(u) - 3)
                        nc.vector.tensor_tensor(inner["rows"][:, ring(u, 4), :, :], gat[:, ring(u, 2), :, :], xb[:, ring(u, 4), :, :], ALU.add)\
                            .then_inc(inner["filled"], 1)
                    u = at(5)
                    if u:
                        ve.wait_ge(beta_done, num(u) + 1)
                        if had(u, 4):
                            ve.wait_ge(outer["normed"], num(u) - 3)
                        nc.vector.tensor_tensor(outer["rows"][:, ring(u, 4), :, :], affine[:, ring(u, 2), :, :], xin[:, ring(u, 8), :, :], ALU.add)\
                            .then_inc(outer["filled"], 1)
                    u = at(6)
                    if u:
                        norm_merge(ve, outer, u, spare_ve)
                run_steps(ve, UNITS, 7, body)

            @blk.tensor
            def _(pe):
                def body(at):
                    u = at(1)
                    if not u:
                        return
                    r = ring(u, 4)
                    pe.wait_ge(hot_ready, num(u) + 1)
                    pe.wait_ge(weighed, num(u) + 1)
                    for h in range(2):
                        pe.wait_ge(part_in[r][h], turn(u, 4) * 16 + 16)
                    if had(u, 4):
                        pe.wait_ge(gat_done, num(u) - 3)
                    for h in range(2):
                        nc.tensor.matmul(agg[r][:, h, 0:D], hot[:, ring(u, 2), h, :], weighted[:, ring(u, 2), h, :], start=True, stop=True)
                        last = nc.tensor.matmul(agg[r][:, h, D:D + H], hot[:, ring(u, 2), h, :], part[:, r, h, H:2 * H],
                                                start=True, stop=True)
                    last.then_inc(summed, 1)
                run_steps(pe, UNITS, 1, body)

            @blk.scalar
            def _(act):
                def body(at):
                    u = at(4)
                    if u:
                        norm_root(act, inner, u)
                    u = at(6)
                    if u:
                        norm_root(act, outer, u)
                    u = at(7)
                    if u:
                        if had(u, 4):
                            act.wait_ge(stored[ring(u, 4)], turn(u, 4) * 16)
                        norm_apply(act, outer, u, x3[:, ring(u, 4), :, :])
                    u = at(8)
                    if u:
                        act.wait_ge(outer["normed"], num(u) + 1)
                        act.dma_start(unit_rows(x3_d, u), x3[:, ring(u, 4), :, :]).then_inc(stored[ring(u, 4)], 16)
                run_steps(act, UNITS, 8, body)
                for k in range(4):
                    act.wait_ge(stored[k], 16 * (UNITS // 4))

    def edges3(sb, ps, sem, sems, block):
        cur = sb("cur", [P, 4, 2], I32)
        xg = sb("xg", [P, 4, 2, D])
        attr = sb("attr", [P, 4, D])
        xT = sb("xT", [P, 2, 3, KC, P])
        qe = sb("qe", [P, 2, 2 * D])
        kv = sb("kv", [P, 4, 2, D])
        prod = sb("prod", [P, 2, D])
        dots = sb("dots", [P, 4, H])
        x_ps = [ps(f"x_ps{k}") for k in range(2)]
        e_ps = [ps(f"e_ps{k}") for k in range(2)]
        qe_ps = [ps(f"qe_ps{k}") for k in range(2)]
        kv_ps = [ps(f"kv_ps{k}") for k in range(2)]
        spare_gp, index, src_in, dst_in = sem("spare_gp"), sem("index"), sems("src_in", 4), sems("dst_in", 4)
        attr_in, attr_in2, stored = sems("attr_in", 4), sems("attr_in2", 4), sems("stored", 4)
        turned, copied, qe_done, kv_done, qe_copied = sem("turned"), sem("copied"), sem("qe_done"), sem("kv_done"), sem("qe_copied")
        joined, prodded, dotted, placed = sem("joined"), sem("prodded"), sem("dotted"), sem("placed")
        cleared = sem("cleared")
        out_rows = by_column(msg3_d)
        edge_attr = a["edge_attr_256"]
        short = E - (P - 1) * EC
        split = P - 16

        with block() as blk:
            @blk.gpsimd
            def _(gp):
                def body(at):
                    c = at(0)
                    r = ring(c, 4)
                    if had(c, 4):
                        gate(gp, spare_gp, turned, num(c) - 3)
                    gp.tensor_copy(cur[:, r, :], edge_rows[:, bass.ds(num(c), 1), :].rearrange("p c w -> p (c w)")).then_inc(index, 1)
                    gate(gp, spare_gp, index, num(c) + 1)
                    for k, arrived in enumerate((src_in, dst_in)):
                        gp.indirect_dma_start(out=xg[:, r, k, :], out_offset=None, in_=x3_d,
                                              in_offset=bass.IndirectOffsetOnAxis(ap=cur[:, r, k:k + 1], axis=0))\
                          .then_inc(arrived[r], 16)
                run_steps(gp, EC, 0, body)

            @blk.sync
            def _(sp):
                def load(c, last_rows):
                    r = ring(c, 4)
                    if had(c, 4):
                        sp.wait_ge(turned, num(c) - 3)
                    for p0, n, arrived in ((0, split, attr_in), (split, last_rows, attr_in2)):
                        sp.dma_start(attr[p0:p0 + n, r, :],
                                     bass.AP(edge_attr.tensor, (num(c) + p0 * EC) * D, [[EC * D, n], [1, D]])).then_inc(arrived[r], 16)
                run_range(sp, 0, short, lambda c: load(c, 16))
                run_range(sp, short, EC, lambda c: load(c, 15))

            @blk.tensor
            def _(pe):
                def body(at):
                    c = at(1)
                    if c:
                        r, b = ring(c, 4), ring(c, 2)
                        for s in (src_in, dst_in, attr_in, attr_in2):
                            pe.wait_ge(s[r], turn(c, 4) * 16 + 16)
                        if had(c, 2):
                            pe.wait_ge(copied, num(c) - 1)
                        for k in range(2):
                            for j in range(KC):
                                nc.tensor.transpose(x_ps[b][:, (k * KC + j) * P:(k * KC + j + 1) * P],
                                                    xg[:, r, k, j * P:(j + 1) * P], ident[:, :])
                        for j in range(KC):
                            last = nc.tensor.transpose(e_ps[b][:, j * P:(j + 1) * P], attr[:, r, j * P:(j + 1) * P], ident[:, :])
                        last.then_inc(turned, 1)
                    c = at(2)
                    if c:
                        b = ring(c, 2)
                        pe.wait_ge(copied, num(c) + 1)
                        if had(c, 2):
                            pe.wait_ge(qe_copied, num(c) - 1)
                        nc.tensor.matmul(qe_ps[b][:, 0:D], ones3[:, :], bias3[:, 2 * D:3 * D], start=True, stop=False)
                        for j in range(KC):
                            nc.tensor.matmul(qe_ps[b][:, 0:D], xT[:, b, 1, j, :], w3_q[:, j, :], start=False, stop=j == KC - 1)
                        for j in range(KC):
                            last = nc.tensor.matmul(qe_ps[b][:, D:2 * D], xT[:, b, 2, j, :], w3_e[:, j, :], start=j == 0, stop=j == KC - 1)
                        last.then_inc(qe_done, 1)
                        if had(c, 2):
                            pe.wait_ge(joined, num(c) - 1)
                        nc.tensor.matmul(kv_ps[b][:, :], ones3[:, :], bias3[:, 0:2 * D], start=True, stop=False)
                        for j in range(KC):
                            last = nc.tensor.matmul(kv_ps[b][:, :], xT[:, b, 0, j, :], w3_kv[:, j, :], start=False, stop=j == KC - 1)
                        last.then_inc(kv_done, 1)
                run_steps(pe, EC, 2, body)

            @blk.scalar
            def _(act):
                def body(at):
                    c = at(1)
                    if c:
                        b = ring(c, 2)
                        act.wait_ge(turned, num(c) + 1)
                        if had(c, 2):
                            act.wait_ge(kv_done, num(c) - 1)
                        nc.scalar.activation(xT[:, b, 0:2, :, :].rearrange("p k j e -> p (k j e)"), x_ps[b][:, :], ACT.Copy)
                        nc.scalar.activation(xT[:, b, 2, :, :].rearrange("p j e -> p (j e)"), e_ps[b][:, 0:D], ACT.Copy)\
                            .then_inc(copied, 1)
                    c = at(2)
                    if c:
                        b = ring(c, 2)
                        act.wait_ge(qe_done, num(c) + 1)
                        if had(c, 2):
                            act.wait_ge(prodded, num(c) - 1)
                        nc.scalar.activation(qe[:, b, :], qe_ps[b][:, :], ACT.Copy).then_inc(qe_copied, 1)
                    c = at(4)
                    if c:
                        act.wait_ge(joined, num(c) + 1)
                        act.dma_start(out_rows[:, bass.ds(num(c), 1), :].rearrange("p c w -> p (c w)"), kv[:, ring(c, 4), 1, :])\
                           .then_inc(stored[ring(c, 4)], 16)
                run_steps(act, EC, 4, body)
                for k in range(4):
                    act.wait_ge(stored[k], 16 * (EC // 4))

            @blk.vector
            def _(ve):
                def body(at):
                    c = at(3)
                    if c:
                        ve.wait_ge(joined, num(c) + 1)
                        if had(c, 2):
                            ve.wait_ge(dotted, num(c) - 1)
                        nc.vector.tensor_tensor(prod[:, ring(c, 2), :], kv[:, ring(c, 4), 0, :], qe[:, ring(c, 2), 0:D], ALU.mult)\
                            .then_inc(prodded, 1)
                    c = at(4)
                    if c:
                        ve.wait_ge(dotted, num(c) + 1)
                        nc.vector.tensor_scalar(scores[:, bass.ds(num(c), 1), :].rearrange("p c w -> p (c w)"), dots[:, ring(c, 4), :],
                                                float(C) ** -0.5, None, ALU.mult).then_inc(placed, 1)
                    c = at(2)
                    if c:
                        b, r = ring(c, 2), ring(c, 4)
                        ve.wait_ge(kv_done, num(c) + 1)
                        ve.wait_ge(qe_copied, num(c) + 1)
                        if had(c, 4):
                            ve.wait_ge(stored[r], turn(c, 4) * 16)
                            ve.wait_ge(prodded, num(c) - 3)
                        nc.vector.tensor_tensor(kv[:, r, :, :], kv_ps[b][:, :].rearrange("p (k w) -> p k w", k=2),
                                                qe[:, b, D:2 * D].unsqueeze(1).to_broadcast([P, 2, D]), ALU.add).then_inc(joined, 1)
                    c = at(3)
                    if c:
                        ve.wait_ge(prodded, num(c) + 1)
                        if had(c, 4):
                            ve.wait_ge(placed, num(c) - 3)
                        nc.vector.tensor_reduce(dots[:, ring(c, 4), :], prod[:, ring(c, 2), :].rearrange("p (h c) -> p h c", h=H),
                                                axis=AX.X, op=ALU.add).then_inc(dotted, 1)
                run_steps(ve, EC, 4, body)

    def nodes3(sb, ps, sem, sems, block):
        xin = sb("xin", [P, 4, 2, D])
        msg = sb("msg", [P, 4, 2, D])
        part = sb("part", [P, 4, 2, H])
        xb = sb("xb", [P, 4, 2, D])
        hot = sb("hot", [P, 2, 2, P])
        weighted = sb("weighted", [P, 2, 2, D])
        xT = sb("xT", [P, 2, KC, 2, P])
        y = sb("y", [P, 4, 2, D])
        ln = norm_buffers(sb, sem, "ln")
        agg = [ps(f"agg{k}") for k in range(2)]
        xT_ps = [ps(f"xT_ps{k}") for k in range(2)]
        x_in, msg_in, part_in, stored = (sems("x_in", 4), [sems(f"msg_in{k}", 2) for k in range(4)],
                                         [sems(f"part_in{k}", 2) for k in range(4)], sems("stored", 4))
        hot_ready, weighed, biased, x_turned, x_copied, summed, spare_ve = (
            sem("hot_ready"), sem("weighed"), sem("biased"), sem("x_turned"), sem("x_copied"), sem("summed"), sem("spare_ve"))

        with block() as blk:
            @blk.sync
            def _(sp):
                def body(at):
                    u = at(0)
                    r = ring(u, 4)
                    if had(u, 4):
                        sp.wait_ge(biased, num(u) - 3)
                        sp.wait_ge(x_turned, num(u) - 3)
                        sp.wait_ge(weighed, num(u) - 3)
                    load_unit(sp, u, xin[:, r, :, :], x3_d, x_in[r])
                    load_windows(sp, u, [(msg3_d, msg[:, r, :, :], msg_in[r]), (share3_d, part[:, r, :, :], part_in[r])])
                run_steps(sp, UNITS, 0, body)

            @blk.gpsimd
            def _(gp):
                def body(at):
                    u = at(0)
                    gp.wait_ge(x_in[ring(u, 4)], turn(u, 4) * 16 + 16)
                    if had(u, 4):
                        gp.wait_ge(ln["filled"], num(u) - 3)
                    gp.tensor_tensor(xb[:, ring(u, 4), :, :], xin[:, ring(u, 4), :, :], both(rows["L3_gnn_bs"]), ALU.add)\
                      .then_inc(biased, 1)
                run_steps(gp, UNITS, 0, body)

            @blk.vector
            def _(ve):
                def body(at):
                    u = at(4)
                    if u:
                        norm_invert(ve, ln, u)
                    u = at(0)
                    if u:
                        one_hot(ve, u, hot, hot_ready, summed, None)
                    u = at(3)
                    if u:
                        norm_measure(ve, ln, u)
                    u = at(4)
                    if u:
                        norm_shift(ve, ln, u)
                    u = at(0)
                    if u:
                        r = ring(u, 4)
                        for h in range(2):
                            ve.wait_ge(msg_in[r][h], turn(u, 4) * 16 + 16)
                            ve.wait_ge(part_in[r][h], turn(u, 4) * 16 + 16)
                        if had(u, 2):
                            ve.wait_ge(summed, num(u) - 1)
                        nc.vector.tensor_tensor(by_head(weighted[:, ring(u, 2), :, :]), by_head(msg[:, r, :, :]),
                                                over_head(part[:, r, :, :]), ALU.mult).then_inc(weighed, 1)
                    u = at(3)
                    if u:
                        norm_merge(ve, ln, u, spare_ve)
                    u = at(2)
                    if u:
                        ve.wait_ge(summed, num(u) + 1)
                        ve.wait_ge(biased, num(u) + 1)
                        if had(u, 4):
                            ve.wait_ge(ln["normed"], num(u) - 3)
                        nc.vector.tensor_tensor(ln["rows"][:, ring(u, 4), :, :], agg[ring(u, 2)][:, :].rearrange("p (h w) -> p h w", h=2),
                                                xb[:, ring(u, 4), :, :], ALU.add).then_inc(ln["filled"], 1)
                run_steps(ve, UNITS, 4, body)

            @blk.tensor
            def _(pe):
                def body(at):
                    u = at(0)
                    if u:
                        pe.wait_ge(x_in[ring(u, 4)], turn(u, 4) * 16 + 16)
                        if had(u, 2):
                            pe.wait_ge(x_copied, num(u) - 1)
                        for k in range(KC):
                            for h in range(2):
                                last = nc.tensor.transpose(xT_ps[ring(u, 2)][:, (k * 2 + h) * P:(k * 2 + h + 1) * P],
                                                           xin[:, ring(u, 4), h, k * P:(k + 1) * P], ident[:, :])
                        last.then_inc(x_turned, 1)
                    u = at(1)
                    if u:
                        b = ring(u, 2)
                        pe.wait_ge(x_copied, num(u) + 1)
                        pe.wait_ge(hot_ready, num(u) + 1)
                        pe.wait_ge(weighed, num(u) + 1)
                        if had(u, 2):
                            pe.wait_ge(ln["filled"], num(u) - 1)
                        for h in range(2):
                            to = agg[b][:, h * D:(h + 1) * D]
                            for k in range(KC):
                                nc.tensor.matmul(to, xT[:, b, k, h, :], w3_s[:, k, :], start=k == 0, stop=False)
                            last = nc.tensor.matmul(to, hot[:, b, h, :], weighted[:, b, h, :], start=False, stop=True)
                        last.then_inc(summed, 1)
                run_steps(pe, UNITS, 1, body)

            @blk.scalar
            def _(act):
                def body(at):
                    u = at(0)
                    if u:
                        b = ring(u, 2)
                        act.wait_ge(x_turned, num(u) + 1)
                        if had(u, 2):
                            act.wait_ge(summed, num(u) - 1)
                        nc.scalar.activation(xT[:, b, :, :, :].rearrange("p k h n -> p (k h n)"), xT_ps[b][:, :], ACT.Copy)\
                            .then_inc(x_copied, 1)
                    u = at(3)
                    if u:
                        norm_root(act, ln, u)
                    u = at(4)
                    if u:
                        if had(u, 4):
                            act.wait_ge(stored[ring(u, 4)], turn(u, 4) * 16)
                        norm_apply(act, ln, u, y[:, ring(u, 4), :, :])
                    u = at(5)
                    if u:
                        act.wait_ge(ln["normed"], num(u) + 1)
                        if is_last(u, UNITS):
                            act.dma_start(out[(TILES - 2) * P:N, :], y[0:LAST_ROWS, ring(u, 4), 0, :]).then_inc(stored[ring(u, 4)], 16)
                        else:
                            act.dma_start(unit_rows(out[0:(UNITS - 1) * 2 * P, :], u), y[:, ring(u, 4), :, :]).then_inc(stored[ring(u, 4)], 16)
                run_steps(act, UNITS, 5, body)
                for k in range(4):
                    act.wait_ge(stored[k], 16 * (UNITS // 4))

    def layer2_edges():
        with ExitStack() as ctx:
            self_scores = ctx.enter_context(nc.sbuf_tensor("self_scores", [P, EC, H], F32))
            stage(lambda *tools: edges2(*tools, self_scores), "edges2")
            stage(lambda *tools: shares(*tools, self_scores, share2_d, 2 * H), "shares2")

    stage(prepare, "prepare")
    stage(edges0, "edges0")
    stage(turn_windows, "turn")
    stage(nodes0, "nodes0")
    stage(nodes1, "nodes1")
    layer2_edges()
    stage(nodes2, "nodes2")
    stage(edges3, "edges3")
    stage(lambda *tools: shares(*tools, None, share3_d, H), "shares3")
    stage(nodes3, "nodes3")


_INS = ["x", "src", "dst", "edge_attr_256", "L0_gnn_Wq", "L0_gnn_Wk", "L0_gnn_Wv", "L1_gnn_W1", "L1_gnn_b1", "L1_gnn_W2",
        "L1_gnn_b2", "L1_gnn_eps", "L1_gnn_gamma", "L1_gnn_beta", "L2_gnn_W", "L2_gnn_att_src", "L2_gnn_att_dst",
        "L2_gnn_bias", "L2_gnn_ln_w", "L2_gnn_ln_b", "L3_gnn_Wq", "L3_gnn_bq", "L3_gnn_Wk", "L3_gnn_bk", "L3_gnn_Wv",
        "L3_gnn_bv", "L3_gnn_We", "L3_gnn_Ws", "L3_gnn_bs"]


def kernel(**inputs):
    import numpy as np
    from concourse import bacc
    from concourse.bass_utils import run_bass_kernel_spmd

    nc = bacc.Bacc("TRN2", target_bir_lowering=False, num_devices=1)
    arrays, args = {}, {}
    for name in _INS:
        value = np.ascontiguousarray(inputs[name])
        shape = value.shape if value.ndim and name not in ("L2_gnn_att_src", "L2_gnn_att_dst") else (value.size,)
        arrays["in_" + name] = value.reshape(shape)
        args[name] = nc.dram_tensor("in_" + name, shape, mybir.dt.from_np(value.dtype), kind="ExternalInput").ap()
    out = nc.dram_tensor("out", (N, D), F32, kind="ExternalOutput").ap()
    build(nc, args, out)
    r = run_bass_kernel_spmd(nc, [arrays], core_ids=[0])
    return r.results[0]["out"]
```
